# Optimizing a Trainium2 kernel written in Bass

```python
import numpy as np
import jax
import jax.numpy as jnp

def _softmax(x, axis=-1):
    return jax.nn.softmax(x, axis=axis)

def _gelu(x):
    return jax.nn.gelu(x, approximate=True)

def _silu(x):
    return jax.nn.silu(x)

def _sigmoid(x):
    return jax.nn.sigmoid(x)

def _layernorm(x, axis=-1, eps=1e-05):
    m = jnp.mean(x, axis=axis, keepdims=True)
    v = jnp.var(x, axis=axis, keepdims=True)
    return (x - m) / jnp.sqrt(v + eps)

def _scatter_add(tgt, idx, src, axis=0):
    return tgt.at[idx].add(src)

def _segment_sum(src, seg, n):
    return jax.ops.segment_sum(src, seg, n)
kernel_name = 'mk_macaron_d1_jaxref_r8_3975e0'

def setup_inputs(seed: int=0):
    np.random.seed(seed)
    _w = jnp.asarray

    def _L0_attn_setup():
        import jax, jax.numpy as jnp
        import numpy as np
        HEADS = 16
        KV_HEADS = 4
        DIM_HEAD = 128
        DIM = 256
        ROPE_BASE = 10000.0

        def rotate_half(t):
            t1, t2 = jnp.split(t, 2, axis=-1)
            return jnp.concatenate((-t2, t1), axis=-1)

        def apply_rotary(t, cos, sin):
            return t * cos + rotate_half(t) * sin
        key = jax.random.key(seed)
        ks = jax.random.split(key, 6)
        b, n = (4, 128)
        s = 1.0 / np.sqrt(DIM)
        x = jax.random.normal(ks[0], (b, n, DIM), dtype=jnp.float32)
        Wq = jax.random.normal(ks[1], (DIM, HEADS * DIM_HEAD), dtype=jnp.float32) * s
        Wk = jax.random.normal(ks[2], (DIM, KV_HEADS * DIM_HEAD), dtype=jnp.float32) * s
        Wv = jax.random.normal(ks[3], (DIM, KV_HEADS * DIM_HEAD), dtype=jnp.float32) * s
        Wo = jax.random.normal(ks[4], (HEADS * DIM_HEAD, DIM), dtype=jnp.float32) * s
        head_scale = 1.0 + 0.02 * jax.random.normal(ks[5], (1, HEADS, 1, 1), dtype=jnp.float32)
        return {'x': x, 'Wq': Wq, 'Wk': Wk, 'Wv': Wv, 'Wo': Wo, 'head_scale': head_scale}
    _L0_attn_in = _L0_attn_setup()

    def _L0_ffn_setup():
        import jax, jax.numpy as jnp
        import numpy as np
        D_MODEL = 256
        D_EXPERT = 1024
        EPS = 1e-08

        def ternary_quant(w):
            scale = jnp.mean(jnp.abs(w)) + EPS
            q = jnp.clip(jnp.round(w / scale), -1.0, 1.0) * scale
            return w + jax.lax.stop_gradient(q - w)
        key = jax.random.key(seed)
        k_x, k_up, k_gate, k_down = jax.random.split(key, 4)
        std_in = 1.0 / np.sqrt(D_MODEL)
        std_exp = 1.0 / np.sqrt(D_EXPERT)
        return {'x': jax.random.normal(k_x, (4, 256, D_MODEL), dtype=jnp.float32), 'W_up': jax.random.normal(k_up, (D_EXPERT, D_MODEL), dtype=jnp.float32) * std_in, 'W_gate': jax.random.normal(k_gate, (D_EXPERT, D_MODEL), dtype=jnp.float32) * std_in, 'W_down': jax.random.normal(k_down, (D_MODEL, D_EXPERT), dtype=jnp.float32) * std_exp}
    _L0_ffn_in = _L0_ffn_setup()
    _d = {'L0_attn_x': _L0_attn_in['x'], 'L0_attn_Wq': _L0_attn_in['Wq'], 'L0_attn_Wk': _L0_attn_in['Wk'], 'L0_attn_Wv': _L0_attn_in['Wv'], 'L0_attn_Wo': _L0_attn_in['Wo'], 'L0_attn_head_scale': _L0_attn_in['head_scale'], 'L0_ffn_W_up': _L0_ffn_in['W_up'], 'L0_ffn_W_gate': _L0_ffn_in['W_gate'], 'L0_ffn_W_down': _L0_ffn_in['W_down']}
    _x0 = _d['L0_attn_x']
    _d['L0_attn_x'] = jax.random.normal(jax.random.fold_in(jax.random.key(seed), 1), (16, 256, 256), dtype=_x0.dtype)
    del _x0
    return _d

def reference(L0_attn_x, L0_attn_Wq, L0_attn_Wk, L0_attn_Wv, L0_attn_Wo, L0_attn_head_scale, L0_ffn_W_up, L0_ffn_W_gate, L0_ffn_W_down):

    def _L0_attn_ref(x, Wq, Wk, Wv, Wo, head_scale):
        import jax, jax.numpy as jnp
        import numpy as np
        HEADS = 16
        KV_HEADS = 4
        DIM_HEAD = 128
        DIM = 256
        ROPE_BASE = 10000.0

        def rotate_half(t):
            t1, t2 = jnp.split(t, 2, axis=-1)
            return jnp.concatenate((-t2, t1), axis=-1)

        def apply_rotary(t, cos, sin):
            return t * cos + rotate_half(t) * sin
        b, n, _ = x.shape
        q = (x @ Wq).reshape(b, n, HEADS, DIM_HEAD).transpose(0, 2, 1, 3)
        k = (x @ Wk).reshape(b, n, KV_HEADS, DIM_HEAD).transpose(0, 2, 1, 3)
        v = (x @ Wv).reshape(b, n, KV_HEADS, DIM_HEAD).transpose(0, 2, 1, 3)
        inv_freq = 1.0 / ROPE_BASE ** (jnp.arange(0, DIM_HEAD, 2, dtype=jnp.float32) / DIM_HEAD)
        freqs = jnp.arange(n, dtype=jnp.float32)[:, None] * inv_freq[None, :]
        emb = jnp.concatenate((freqs, freqs), axis=-1)
        cos, sin = (jnp.cos(emb), jnp.sin(emb))
        q = apply_rotary(q, cos, sin)
        k = apply_rotary(k, cos, sin)
        rep = HEADS // KV_HEADS
        k = jnp.repeat(k, rep, axis=1)
        v = jnp.repeat(v, rep, axis=1)
        scale = 1.0 / jnp.sqrt(jnp.array(DIM_HEAD, dtype=x.dtype))
        scores = jnp.einsum('bhid,bhjd->bhij', q, k) * scale
        causal = jnp.tril(jnp.ones((n, n), dtype=bool))
        scores = jnp.where(causal, scores, jnp.finfo(scores.dtype).min)
        attn = jax.nn.softmax(scores, axis=-1)
        out = jnp.einsum('bhij,bhjd->bhid', attn, v)
        out = out * head_scale
        out = out.transpose(0, 2, 1, 3).reshape(b, n, HEADS * DIM_HEAD)
        return out @ Wo

    def _L0_ffn_ref(x, W_up, W_gate, W_down):
        import jax, jax.numpy as jnp
        import numpy as np
        D_MODEL = 256
        D_EXPERT = 1024
        EPS = 1e-08

        def ternary_quant(w):
            scale = jnp.mean(jnp.abs(w)) + EPS
            q = jnp.clip(jnp.round(w / scale), -1.0, 1.0) * scale
            return w + jax.lax.stop_gradient(q - w)
        wu = ternary_quant(W_up)
        wg = ternary_quant(W_gate)
        wd = ternary_quant(W_down)
        up = jnp.einsum('bsd,ed->bse', x, wu)
        gate = jnp.einsum('bsd,ed->bse', x, wg)
        hidden = jax.nn.silu(up) * gate
        return jnp.einsum('bse,de->bsd', hidden, wd)
    x = L0_attn_x
    x = x + 0.5 * _L0_ffn_ref(_layernorm(x, axis=-1), L0_ffn_W_up, L0_ffn_W_gate, L0_ffn_W_down)
    x = x + _L0_attn_ref(_layernorm(x, axis=-1), L0_attn_Wq, L0_attn_Wk, L0_attn_Wv, L0_attn_Wo, L0_attn_head_scale)
    x = x + 0.5 * _L0_ffn_ref(_layernorm(x, axis=-1), L0_ffn_W_up, L0_ffn_W_gate, L0_ffn_W_down)
    return x

_drawn_inputs = setup_inputs


def setup_inputs(seed=0):
    import zlib

    import numpy as np

    out = dict(_drawn_inputs(seed))
    spreads = {}
    factors = {}
    for name, (base, spread) in spreads.items():
        noise = np.random.default_rng([zlib.crc32(name.encode()), seed]).standard_normal(out[name].shape)
        drawn = base * np.exp(spread * noise) if base else spread * noise
        out[name] = jnp.asarray(drawn.astype(out[name].dtype))
    for name, factor in factors.items():
        out[name] = (out[name] * factor).astype(out[name].dtype)
    return out
```

```python
from contextlib import ExitStack

import numpy as np

import concourse.bass as bass
from concourse import mybir

F32 = mybir.dt.float32
F16 = mybir.dt.float16
BF16 = mybir.dt.bfloat16
ALU = mybir.AluOpType
ACT = mybir.ActivationFunctionType
AX = mybir.AxisListType

BATCH, SEQ, D = 16, 256, 256
HEADS, KV, DH = 16, 4, 128
E = 1024
TOK = BATCH * SEQ
P = 128
DC = D // P
FC = E // P
TILE = 512
TILES = TOK // TILE
SUB = TILE // P
PAIRS = HEADS // 2
UNITS = 2 * BATCH
STEPS = BATCH * PAIRS
EPS = 1e-5
LNS = 16.0
WTOP = 1024.0
VS = 2.0 ** -8
HSC = 2.0 ** -5
MASKED = -1e30


def program(nc, x, wq, wk, wv, wo, hscale, wu, wg, wd, cos_t, sin_t, out):
    ctx = ExitStack()
    with ctx:
        def sb(name, shape, dt):
            return ctx.enter_context(nc.sbuf_tensor(name, shape, dt))

        def pb(name):
            return ctx.enter_context(nc.psum_tensor(name, [P, 512], F32))

        def sem(name):
            return ctx.enter_context(nc.semaphore(name))

        X = sb("X", [P, TOK // P * D], F32)
        XH = sb("XH", [P, DC, TOK], F16)
        XL = sb("XL", [P, DC, TOK], F16)
        TU = sb("TU", [P, DC, E], F16)
        TG = sb("TG", [P, DC, E], F16)
        TD = sb("TD", [P, FC, D], F16)
        WQH, WQL = (sb(n, [P, DC, HEADS * DH], F16) for n in ("WQH", "WQL"))
        WKH, WKL = (sb(n, [P, DC, KV * DH], F16) for n in ("WKH", "WKL"))
        WVH, WVL = (sb(n, [P, DC, KV * DH], F16) for n in ("WVH", "WVL"))
        WOH, WOL = (sb(n, [P, HEADS, D], F16) for n in ("WOH", "WOL"))
        ARENA = sb("ARENA", [P, 10240], F32)
        RU, RG, RD = (ARENA[:, i * 2048:(i + 1) * 2048] for i in range(3))
        RQ, RK, RV, RO = ARENA[:, 0:4096], ARENA[:, 4096:5120], ARENA[:, 5120:6144], ARENA[:, 6144:10240]
        OH = ARENA[:, 0:4096].bitcast(F16)
        OL = ARENA[:, 4096:8192].bitcast(F16)
        IDF = sb("IDF", [P, P], F32)
        IDB = sb("IDB", [P, P], BF16)
        MASK = sb("MASK", [P, P], BF16)
        SCR = sb("SCR", [P, 7680], F32)
        SG = SCR[:, 0:1024].rearrange("p (b n) -> p b n", b=2)
        H32 = SCR[:, 1024:2048].rearrange("p (b n) -> p b n", b=2)
        HH = SCR[:, 2048:3072].bitcast(F16).rearrange("p (b n) -> p b n", b=4)
        HL = SCR[:, 3072:4096].bitcast(F16).rearrange("p (b n) -> p b n", b=4)
        XN = SCR[:, 4096:5120].rearrange("p (s n) -> p s n", s=4)
        M1 = SCR[:, 0:1024].rearrange("p (b n) -> p b n", b=2)
        M2 = SCR[:, 1024:2048].rearrange("p (b n) -> p b n", b=2)
        Q32 = SCR[:, 2048:3072].rearrange("p (b n) -> p b n", b=2)
        K32 = SCR[:, 3072:3584]
        V32 = SCR[:, 3584:4096].rearrange("p (j n) -> p j n", j=2)
        EX = SCR[:, 4096:5632].rearrange("p (b h n) -> p b h n", b=2, h=2)
        PT = SCR[:, 5632:7168].rearrange("p (b h n) -> p b h n", b=2, h=2)
        XN2 = SCR[:, 7168:7424]
        COS = sb("COS", [P, 256], F32)
        SIN = sb("SIN", [P, 256], F32)
        ST = sb("ST", [P, 4, 6], F32)
        MV = sb("MV", [P, 4, 2], F32)
        VE = sb("VE", [P, 4], F32)
        RSTD = sb("RSTD", [P, 4], F32)
        NEGHALF = sb("NEGHALF", [P, 4], F32)
        HS = sb("HS", [P, HEADS], F32)
        PSUMS = sb("PSUMS", [P, 4], F32)
        FSC = sb("FSC", [P, 4], F32)
        FHALF = sb("FHALF", [P, 4], F32)
        FNEG = sb("FNEG", [P, 4], F32)
        FREC = sb("FREC", [P, 4], F32)
        SU16 = sb("SU16", [P, 1], F32)
        CS = sb("CS", [P, 1], F32)
        CY0 = sb("CY0", [P, 1], F32)
        CY = sb("CY", [P, 1], F32)
        PMAX = sb("PMAX", [P, 4], F32)
        AMAX = sb("AMAX", [P, 4], F32)
        AMG = sb("AMG", [P, 4], F32)
        AREC = sb("AREC", [P, 4], F32)
        AFAC = sb("AFAC", [P, 4], F32)
        SCQ0 = sb("SCQ0", [P, 1], F32)
        SCQ = sb("SCQ", [P, 1], F32)
        CW0 = sb("CW0", [P, 1], F32)
        CW = sb("CW", [P, 1], F32)
        NM = sb("NM", [P, 2, 4], F32)
        RS = sb("RS", [P, 2, 4], F32)
        RI = sb("RI", [P, 2, 4], F32)

        bank = [pb(f"bank{i}") for i in range(8)]
        UB, GB, YB, TB = bank[0:2], bank[2:4], bank[4:6], bank[6:8]
        PJ, SBK, OB, WB = bank[0:2], bank[2:4], bank[4], bank[5]

        xin = [sem(f"x_in{i}") for i in range(3)]
        ffn_raw, attn_raw, hs_in, tab_in = sem("ffn_raw"), sem("attn_raw"), sem("hs_in"), sem("tab_in")
        consts = sem("consts_ready")
        neghalf = sem("neghalf_ready")
        f_part, f_tot, f_sc, tern_a, tern = (sem(n) for n in ("f_partial", "f_total", "f_scales", "tern_cmp", "ternary_ready"))
        a_sc_dve = sem("a_scale_steps")
        hs_mul, a_part, a_tot, a_sc = sem("wo_head_scaled"), sem("a_partial"), sem("a_total"), sem("a_scales")
        w_scaled, w_hi, w_ready = sem("w_scaled"), sem("w_hi"), sem("attn_weights_ready")
        ln_st, ln_mv, ln_ve, ln_rs, ln_xn, ln_t, ln_xh, ln_xl = (
            sem("ln_" + n) for n in ("stats", "meanvar", "vareps", "rstd", "xn", "turned", "xh", "xl"))
        ff = [{n: sem(f"{n}_{l}") for n in ("u_done", "g_done", "silu_done", "h_done", "hh_done", "hl_done",
                                            "down_done", "y_done", "x_done")} for l in range(2)]
        out_done = sem("out_done")
        proj, mul, vdone, add = sem("proj_done"), sem("rope_mul"), sem("v_done"), sem("rope_add")
        s_done, mx, ex, rcp, pn = sem("scores_done"), sem("max_done"), sem("exp_done"), sem("recip_done"), sem("probs_normed")
        pt_t, pt_c, o_done, oh, ol = sem("probs_turned"), sem("probs_copied"), sem("o_done"), sem("o_hi"), sem("o_lo")
        w_done, x2, a_st, a_mv, a_ve, a_rs, a_xn, a_xh, a_xl = (
            sem("at_" + n) for n in ("wo_done", "x2", "stats", "meanvar", "vareps", "rstd", "xn", "xh", "xl"))

        xv = x.rearrange("b (t p) d -> p (b t) d", p=P)
        ov = out.rearrange("b (t p) d -> p (b t) d", p=P)
        XV = X[:, :].rearrange("p (j d) -> p j d", d=D)

        def wait(eng, s, value):
            if not isinstance(value, int) or value > 0:
                eng.wait_ge(s, value)

        def wait_alone(eng, s, value):
            if not isinstance(value, int):
                value = eng.to_reg(value)
                eng.wait_ge(consts, 6)
            eng.wait_ge(s, value)

        def real(b, i, lag):
            return not isinstance(b, int) or 0 <= PAIRS * b + i - lag < STEPS

        def ln_jobs(n):
            if isinstance(n, int) and n == 0:
                return (1, 1), None
            if isinstance(n, int) and n == TILES - 1:
                return None, (2 * n, n - 1)
            return (2 * n, n + 1), (2 * n + 1, n - 1)

        def post(u):
            w = u - 3
            return None if isinstance(w, int) and not 0 <= w < UNITS else w

        def batches(eng, body):
            body(0)
            body(1)
            with eng.Fori(2, BATCH) as b:
                body(b)
            body(BATCH)

        def extra(u):
            return u - 2 * BATCH

        def for_tiles(eng, body):
            body(0)
            with eng.Fori(1, TILES) as n:
                body(n)

        block = ctx.enter_context(nc.Block())

        @block.sync
        def _(sp):
            sp.dma_start(RU, wu.rearrange("(c p) e -> p c e", p=P)).then_inc(ffn_raw, 16)
            sp.dma_start(XV[:, 0:4, :], xv[:, 0:4, :]).then_inc(xin[0], 16)
            sp.dma_start(RG, wg.rearrange("(c p) e -> p c e", p=P)).then_inc(ffn_raw, 16)
            sp.dma_start(RD, wd.rearrange("(c p) d -> p c d", p=P)).then_inc(ffn_raw, 16)
            sp.dma_start(XV[:, 4:8, :], xv[:, 4:8, :]).then_inc(xin[1], 16)
            sp.dma_start(XV[:, 8:32, :], xv[:, 8:32, :]).then_inc(xin[2], 16)
            sp.dma_start(RO, wo.rearrange("(h p) d -> p h d", p=P)).then_inc(attn_raw, 16)
            sp.wait_ge(tern, 3)
            sp.dma_start(RQ, wq.rearrange("(c p) e -> p c e", p=P)).then_inc(attn_raw, 16)
            sp.dma_start(RK, wk.rearrange("(c p) e -> p c e", p=P)).then_inc(attn_raw, 16)
            sp.dma_start(RV, wv.rearrange("(c p) e -> p c e", p=P)).then_inc(attn_raw, 16)
            with sp.Fori(0, TILES) as n:
                sp.wait_ge(ff[1]["x_done"], n * SUB + SUB)
                sp.dma_start(ov[:, bass.ds(n * SUB, SUB), :], XV[:, bass.ds(n * SUB, SUB), :]).then_inc(out_done, 16)
            sp.wait_ge(out_done, 16 * TILES)

        @block.gpsimd
        def _(gp):
            gp.memset(NEGHALF[:, :], -0.5).then_inc(neghalf, 1)
            gp.memset(IDF[:, :], 0.0).then_inc(consts, 1)
            gp.memset(IDB[:, :], 0.0).then_inc(consts, 1)
            gp.memset(MASK[:, :], 0.0).then_inc(consts, 1)
            gp.wait_ge(consts, 3)
            for m in (IDF, IDB):
                gp.affine_select(out=m[:, :], in_=m[:, :], compare_op=ALU.not_equal, fill=1.0, base=0,
                                 pattern=[[-1, P]], channel_multiplier=1).then_inc(consts, 1)
            gp.affine_select(out=MASK[:, :], in_=MASK[:, :], compare_op=ALU.is_ge, fill=MASKED, base=0,
                             pattern=[[-1, P]], channel_multiplier=1).then_inc(consts, 1)
            gp.wait_ge(f_part, 3)
            gp.partition_all_reduce(FSC[:, 0:3], PSUMS[:, 0:3], P, bass.bass_isa.ReduceOp.add).then_inc(f_tot, 1)

            def rstd(q):
                wait(gp, ln_xn, 4 * q)
                wait_alone(gp, ln_mv, 4 * q + 4)
                gp.tensor_scalar(VE[:, :], MV[:, :, 1], 1.0 / LNS ** 2, EPS / LNS ** 2, ALU.mult, ALU.add).then_inc(ln_ve, 1)
                gp.wait_ge(ln_ve, q + 1)
                gp.tensor_tensor(RSTD[:, :], VE[:, :], NEGHALF[:, :], ALU.pow).then_inc(ln_rs, 1)

            gp.wait_ge(neghalf, 1)
            rstd(0)
            rstd(1)
            gp.wait_ge(a_part, 4)
            gp.partition_all_reduce(AMAX[:, :], PMAX[:, :], P, bass.bass_isa.ReduceOp.max).then_inc(a_tot, 1)
            gp.wait_ge(a_sc, 1)
            mats = [(RQ, WQH, WQL), (RK, WKH, WKL), (RV, WVH, WVL), (RO, WOH, WOL)]
            done = 0
            for i, (raw, hi, lo) in enumerate(mats):
                width = raw.shape[1]
                rv = raw.rearrange("p (c n) -> p c n", c=hi.shape[1])
                gp.tensor_scalar(raw, raw, AFAC[:, i:i + 1], 1.0, ALU.mult, ALU.mult).then_inc(w_scaled, 1)
                gp.wait_ge(w_scaled, i + 1)
                gp.tensor_copy(hi[:, :, :], rv).then_inc(w_hi, 1)
                gp.wait_ge(w_hi, i + 1)
                gp.tensor_tensor(lo[:, :, :], rv, hi[:, :, :], ALU.subtract).then_inc(w_ready, 1)
            with gp.Fori(1, TILES - 1) as n:
                for job, _ in ln_jobs(n):
                    rstd(job)
            rstd(2 * TILES - 2)
            rstd(2 * TILES - 1)

            def rope_add(r, dst, waits):
                gp.wait_ge(mul, r + 1)
                for s, v in waits:
                    wait(gp, s, v)
                gp.tensor_tensor(dst, M1[:, rpar[0], :], M2[:, rpar[0], :], ALU.add).then_inc(add, 1)
                rpar[0] ^= 1

            rpar = [0]

            def rows_rstd(w):
                wait_alone(gp, a_mv, w + 1)
                gp.tensor_scalar(VE[:, 0:1], MV[:, 0, 1:2], 1.0 / LNS ** 2, EPS / LNS ** 2, ALU.mult, ALU.add).then_inc(a_ve, 1)
                gp.wait_ge(a_ve, w + 1)
                gp.tensor_tensor(RSTD[:, 0:1], VE[:, 0:1], NEGHALF[:, 0:1], ALU.pow).then_inc(a_rs, 1)

            def norm(b, i):
                t = PAIRS * b + i - 1
                par = (i - 1) % 2
                wait_alone(gp, rcp, t + 1)
                for hh in range(2):
                    gp.tensor_scalar(EX[:, par, hh, 0:128], EX[:, par, hh, 0:128], RI[:, par, 2 * hh:2 * hh + 1], 1.0, ALU.mult, ALU.mult)
                    gp.tensor_scalar(EX[:, par, hh, 128:384], EX[:, par, hh, 128:384], RI[:, par, 2 * hh + 1:2 * hh + 2], 1.0,
                                     ALU.mult, ALU.mult).then_inc(pn, 1)

            def batch(b):
                rpar[0] = 0
                for i in range(PAIRS):
                    g, k = divmod(i, 4)
                    u = 2 * b + g
                    if real(b, i, 0):
                        if k == 0:
                            rope_add(5 * u, K32, [(s_done, 8 * u)])
                        rope_add(5 * u + 1 + k, Q32[:, i % 2, :], [(s_done, 2 * (PAIRS * b + i) - 2)])
                    if k == 0 and post(u) is not None:
                        rows_rstd(post(u))
                    if real(b, i, 1):
                        norm(b, i)

            batches(gp, batch)
            rows_rstd(post(2 * BATCH + 2))

        @block.scalar
        def _(act):
            act.dma_start(HS[:, :], hscale).then_inc(hs_in, 16)
            act.dma_start(COS[:, :], cos_t).then_inc(tab_in, 16)
            act.dma_start(SIN[:, :], sin_t).then_inc(tab_in, 16)

            def ln_hi(q, tile):
                for c in range(DC):
                    act.wait_ge(ln_t, 2 * q + c + 1)
                    act.copy(XH[:, c, bass.ds(tile * TILE, TILE)], TB[c][:, :]).then_inc(ln_xh, 1)

            def ffn(layer, n, jobs):
                s = ff[layer]
                for f in range(FC):
                    j = FC * n + f
                    act.wait_ge(s["u_done"], j + 1)
                    wait(act, s["h_done"], j - 1)
                    act.activation(SG[:, f % 2, :], UB[f % 2][:, :], ACT.Silu, scale=SU16[:, 0:1]).then_inc(s["silu_done"], 1)
                    act.wait_ge(s["h_done"], j + 1)
                    wait(act, s["down_done"], j - 3)
                    act.copy(HH[:, f % 4, :], H32[:, f % 2, :]).then_inc(s["hh_done"], 1)
                    if f in (3, 6) and jobs[f // 6]:
                        ln_hi(*jobs[f // 6])

            act.wait_ge(f_sc, 3)
            ln_hi(0, 0)
            ffn(0, 0, ln_jobs(0))
            with act.Fori(1, TILES - 1) as n:
                ffn(0, n, ln_jobs(n))
            ffn(0, TILES - 1, ln_jobs(TILES - 1))
            ln_hi(2 * TILES - 1, TILES - 1)

            def batch(b):
                for i in range(PAIRS):
                    g, k = divmod(i, 4)
                    u, t = 2 * b + g, PAIRS * b + i
                    if real(b, i, 1):
                        e, par = t - 1, (i - 1) % 2
                        for hh in range(2):
                            act.wait_ge(mx, 2 * e + hh + 1)
                            wait(act, pt_t, 2 * e - 2)
                            for blk, (lo, hi) in enumerate(((0, 128), (128, 384))):
                                c = 2 * hh + blk
                                last = act.activation(EX[:, par, hh, lo:hi], SBK[hh][:, lo:hi], ACT.Exp,
                                                      bias=NM[:, par, c:c + 1], accum_out=RS[:, par, c:c + 1])
                            last.then_inc(ex, 1)
                    if real(b, i, 3):
                        e = t - 3
                        act.wait_ge(o_done, e + 1)
                        slot = ((b * PAIRS + i - 3) // PAIRS) % 2 if isinstance(b, int) else ((b + (1 if i >= 3 else 0) + 1) % 2)
                        head = 2 * ((i - 3) % PAIRS)
                        act.copy(OH[:, bass.ds(slot * 4096 + head * 256, 512)], OB[:, :]).then_inc(oh, 1)
                    if k == 3 and real(b, i, 0):
                        pass
                    if k == 2 and real(b, i, 0):
                        act.wait_ge(proj, 6 * u + 5)
                        wait(act, o_done, 4 * u)
                        act.mul(V32[:, :, :], PJ[0][:, :], VS).then_inc(vdone, 1)
                    if real(b, i, 2):
                        e, par = t - 2, i % 2
                        for hh in range(2):
                            act.wait_ge(pt_t, 2 * e + hh + 1)
                            wait(act, o_done, e - 1)
                            act.copy(PT[:, par, hh, :], TB[hh][:, 0:384]).then_inc(pt_c, 1)
                            if k == 2 and post(u) is not None:
                                turned(act, b, i, u, hh)
                    elif k == 2 and post(u) is not None:
                        for hh in range(2):
                            act.wait_ge(pt_t, 2 * STEPS + 2 * extra(u) + hh + 1)
                            turned(act, b, i, u, hh)

            def turned(act, b, i, u, c):
                act.copy(XH[:, c, bass.ds(post(u) * P, P)], TB[c][:, 384:512]).then_inc(a_xh, 1)

            batches(act, batch)
            for u in (2 * BATCH + 2,):
                for c in range(DC):
                    act.wait_ge(pt_t, 2 * STEPS + 2 * extra(u) + c + 1)
                    turned(act, BATCH + 1, 2, u, c)

            for_tiles(act, lambda n: ffn(1, n, (None, None)))

        @block.tensor
        def _(pe):
            def turn(q):
                wait(pe, ln_xl, 2 * q)
                for s in range(SUB):
                    pe.wait_ge(ln_xn, 4 * q + s + 1)
                    if s == SUB - 1:
                        break
                for c in range(DC):
                    for s in range(SUB):
                        last = pe.transpose(TB[c][:, s * P:(s + 1) * P], XN[:, s, c * P:(c + 1) * P], IDF[:, :])
                    last.then_inc(ln_t, 1)

            def up(layer, n, f):
                s = ff[layer]
                j = FC * n + f
                cols = bass.ds(n * TILE, TILE)
                wait(pe, s["silu_done"], j - 1)
                for a, xs in enumerate((XH, XL)):
                    for c in range(DC):
                        last = pe.matmul(UB[f % 2][:, :], TU[:, c, f * P:(f + 1) * P], xs[:, c, cols],
                                         start=a + c == 0, stop=a + c == 2)
                last.then_inc(s["u_done"], 1)
                wait(pe, s["h_done"], j - 1)
                for a, xs in enumerate((XH, XL)):
                    for c in range(DC):
                        last = pe.matmul(GB[f % 2][:, :], TG[:, c, f * P:(f + 1) * P], xs[:, c, cols],
                                         start=a + c == 0, stop=a + c == 2)
                last.then_inc(s["g_done"], 1)

            def down(layer, n, f):
                s = ff[layer]
                j = FC * n + f
                pe.wait_ge(s["hl_done"], j + 1)
                if f == 0:
                    wait(pe, s["x_done"], SUB * n)
                for sub in range(SUB):
                    for a, hs in enumerate((HH, HL)):
                        last = pe.matmul(YB[sub // 2][:, (sub % 2) * D:(sub % 2 + 1) * D], hs[:, f % 4, sub * P:(sub + 1) * P],
                                         TD[:, f, :], start=f == 0 and a == 0 and sub % 2 == 0,
                                         stop=f == FC - 1 and a == 1, skip_group_check=True)
                last.then_inc(s["down_done"], 1)

            def ffn(layer, n, jobs, prev):
                for f in range(FC):
                    up(layer, n, f)
                    if f >= 2:
                        down(layer, n, f - 2)
                    elif prev:
                        down(layer, n - 1, f + FC - 2)
                    if f in (2, 6) and jobs[f // 6]:
                        turn(jobs[f // 6][0])

            pe.wait_ge(consts, 6)
            turn(0)
            pe.wait_ge(tern, 3)
            pe.wait_ge(ln_xl, 2)
            ffn(0, 0, ln_jobs(0), False)
            pe.wait_ge(ln_xl, 4)
            ffn(0, 1, ln_jobs(1), True)
            with pe.Fori(2, TILES - 1) as n:
                pe.wait_ge(ln_xl, 4 * n - 2)
                ffn(0, n, ln_jobs(n), True)
            pe.wait_ge(ln_xl, 4 * TILES - 6)
            ffn(0, TILES - 1, ln_jobs(TILES - 1), True)
            down(0, TILES - 1, FC - 2)
            down(0, TILES - 1, FC - 1)
            turn(2 * TILES - 1)

            def three(dst, lh, ll, rh, rl, start, stop):
                first = True
                for a, (l, r) in enumerate(((lh, rh), (lh, rl), (ll, rh))):
                    for c in range(DC):
                        last = pe.matmul(dst, l(c), r(c), start=start and first, stop=stop and a + c == 3, skip_group_check=True)
                        first = False
                return last

            def project_qk(dst, wh, wl, h0, b):
                cols = bass.ds(b * SEQ, SEQ)
                for hh in range(2):
                    w = slice((h0 + hh) * DH, (h0 + hh + 1) * DH)
                    last = three(dst[:, hh * SEQ:(hh + 1) * SEQ], lambda c: wh[:, c, w], lambda c: wl[:, c, w],
                                 lambda c: XH[:, c, cols], lambda c: XL[:, c, cols], hh == 0, hh == 1)
                last.then_inc(proj, 1)

            def project_v(b, g):
                for j in range(2):
                    rows = bass.ds(b * SEQ + j * P, P)
                    w = slice(g * 256, g * 256 + 256)
                    last = three(PJ[0][:, j * 256:(j + 1) * 256], lambda c: XH[:, c, rows], lambda c: XL[:, c, rows],
                                 lambda c: WVH[:, c, w], lambda c: WVL[:, c, w], j == 0, j == 1)
                last.then_inc(proj, 1)

            def scores(b, i):
                t = PAIRS * b + i - 1
                par = (i - 1) % 2
                gg, kk = divmod((i - 1) % PAIRS, 4)
                pe.wait_ge(add, (5 * (2 * b + gg) if i > 0 else 5 * (2 * b - 1)) + kk + 2)
                kv = kk // 2
                for hh in range(2):
                    wait(pe, ex, 2 * t + hh - 1)
                    q = Q32[:, par, hh * SEQ:(hh + 1) * SEQ]
                    kt = K32[:, kv * SEQ:(kv + 1) * SEQ]
                    bk = SBK[hh]
                    pe.matmul(bk[:, 0:128], q[:, 0:128], kt[:, 0:128], start=True, stop=False, skip_group_check=True)
                    pe.matmul(bk[:, 0:128], IDB[:, :], MASK[:, :], start=False, stop=False, skip_group_check=True)
                    pe.matmul(bk[:, 128:384], q[:, 128:256], kt, start=False, stop=False, skip_group_check=True)
                    pe.matmul(bk[:, 256:384], IDB[:, :], MASK[:, :], start=False, stop=True,
                              skip_group_check=True).then_inc(s_done, 1)

            def values(b, i):
                t = PAIRS * b + i - 3
                par = (i - 3) % 2
                gg, kk = divmod((i - 3) % PAIRS, 4)
                kv = kk // 2
                pe.wait_ge(vdone, 2 * b + gg + 1 - (2 if i < 3 else 0))
                wait(pe, ol, t)
                for hh in range(2):
                    pe.wait_ge(pt_c, 2 * t + hh + 1)
                    v = V32[:, :, kv * DH:(kv + 1) * DH]
                    pe.matmul(OB[:, hh * 256:hh * 256 + 256], v[:, 0, :], PT[:, par, hh, 0:256],
                              start=hh == 0, stop=False, skip_group_check=True)
                    last = pe.matmul(OB[:, hh * 256 + 128:hh * 256 + 256], v[:, 1, :], PT[:, par, hh, 256:384],
                                     start=False, stop=hh == 1, skip_group_check=True)
                last.then_inc(o_done, 1)

            def turn_probs(b, i, u):
                t = PAIRS * b + i - 2
                par = i % 2
                rows = i % 4 == 2 and post(u) is not None
                for hh in range(2):
                    wait(pe, pt_c, 2 * t + hh - 1)
                    if i % 4 == 3 and post(u) is not None:
                        pe.wait_ge(a_xl, 2 * post(u) + 2)
                    pe.wait_ge(pn, 2 * t + hh + 1)
                    for blk in range(3):
                        last = pe.transpose(TB[hh][:, blk * P:(blk + 1) * P], EX[:, par, hh, blk * P:(blk + 1) * P], IDF[:, :])
                    if rows:
                        pe.wait_ge(a_xn, post(u) + 1)
                        last = pe.transpose(TB[hh][:, 384:512], XN2[:, hh * P:(hh + 1) * P], IDF[:, :])
                    last.then_inc(pt_t, 1)

            def turn_rows(u):
                wait(pe, pt_c, 2 * STEPS)
                pe.wait_ge(a_xl, 2 * post(u))
                pe.wait_ge(a_xn, post(u) + 1)
                for c in range(DC):
                    pe.transpose(TB[c][:, 384:512], XN2[:, c * P:(c + 1) * P], IDF[:, :]).then_inc(pt_t, 1)

            def output(b, g, k):
                w = 2 * b + g - 2
                pe.wait_ge(ol, PAIRS * (b - 1) + 2 * k + 2)
                if k == 0:
                    wait(pe, x2, w)
                slot = (b - 1) % 2 if isinstance(b, int) else (b + 1) % 2
                for h in range(4 * k, 4 * k + 4):
                    rows = bass.ds(slot * 4096 + h * 256 + g * P, P)
                    for a, (o, wo_) in enumerate(((OH, WOH), (OH, WOL), (OL, WOH))):
                        last = pe.matmul(WB[:, 0:256], o[:, rows], wo_[:, h, :], start=h == 0 and a == 0,
                                         stop=h == HEADS - 1 and a == 2, skip_group_check=True)
                if k == 3:
                    last.then_inc(w_done, 1)

            def batch(b):
                for i in range(PAIRS):
                    g, k = divmod(i, 4)
                    u = 2 * b + g
                    if real(b, i, 1):
                        scores(b, i)
                    if real(b, i, 0):
                        if k == 0:
                            wait(pe, vdone, u)
                            project_qk(PJ[0], WKH, WKL, 2 * g, b)
                        wait(pe, mul, 5 * u + k)
                        project_qk(PJ[(1, 0, 1, 1)[k]], WQH, WQL, 8 * g + 2 * k, b)
                    if real(b, i, 3):
                        values(b, i)
                    if real(b, i, 0) and k == 2:
                        pe.wait_ge(mul, 5 * u + 3)
                        project_v(b, g)
                    if real(b, i, 2):
                        turn_probs(b, i, u)
                    elif k == 2 and post(u) is not None:
                        turn_rows(u)
                    if not isinstance(b, int) or b > 0:
                        output(b, g, k)

            pe.wait_ge(w_ready, 4)
            pe.wait_ge(ln_xl, 4 * TILES)
            batches(pe, batch)
            turn_rows(2 * BATCH + 2)

            pe.wait_ge(a_xl, 2 * UNITS)
            ffn(1, 0, (None, None), False)
            with pe.Fori(1, TILES) as n:
                ffn(1, n, (None, None), True)
            down(1, TILES - 1, FC - 2)
            down(1, TILES - 1, FC - 1)

        @block.vector
        def _(ve):
            def stats(q, tile):
                for s in range(SUB):
                    ve.bn_stats(ST[:, s, :], X[:, bass.ds(tile * (SUB * D) + s * D, D)]).then_inc(ln_st, 1)
                for s in range(SUB):
                    wait_alone(ve, ln_st, 4 * q + s + 1)
                    ve.bn_aggr(MV[:, s, :], ST[:, s, :]).then_inc(ln_mv, 1)

            def center(q, tile):
                ve.wait_ge(ln_rs, q + 1)
                wait(ve, ln_t, 2 * q)
                for s in range(SUB):
                    ve.tensor_scalar(XN[:, s, :], X[:, bass.ds(tile * (SUB * D) + s * D, D)], MV[:, s, 0:1],
                                     RSTD[:, s:s + 1], ALU.subtract, ALU.mult).then_inc(ln_xn, 1)

            def ln_lo(q, tile):
                for c in range(DC):
                    cols = bass.ds(tile * TILE, TILE)
                    ve.wait_ge(ln_xh, 2 * q + c + 1)
                    ve.tensor_tensor(XL[:, c, cols], TB[c][:, :], XH[:, c, cols], ALU.subtract).then_inc(ln_xl, 1)

            def residual(layer, tile):
                s = ff[layer]
                ve.wait_ge(s["down_done"], FC * tile + FC)
                for sub in range(SUB):
                    rows = X[:, bass.ds(tile * (SUB * D) + sub * D, D)]
                    ve.scalar_tensor_tensor(rows, YB[sub // 2][:, (sub % 2) * D:(sub % 2 + 1) * D], CY[:, 0:1], rows,
                                            ALU.mult, ALU.add).then_inc(s["x_done"], 1)

            def lo(layer, n, f):
                s = ff[layer]
                ve.wait_ge(s["hh_done"], FC * n + f + 1)
                ve.tensor_tensor(HL[:, f % 4, :], H32[:, f % 2, :], HH[:, f % 4, :], ALU.subtract).then_inc(s["hl_done"], 1)

            def ffn(layer, n, jobs, prev):
                s = ff[layer]
                ahead, behind = jobs
                for f in range(FC):
                    j = FC * n + f
                    ve.wait_ge(s["silu_done"], j + 1)
                    ve.wait_ge(s["g_done"], j + 1)
                    wait(ve, s["hl_done"], j - 1)
                    ve.scalar_tensor_tensor(H32[:, f % 2, :], SG[:, f % 2, :], CS[:, 0:1], GB[f % 2][:, :],
                                            ALU.mult, ALU.mult).then_inc(s["h_done"], 1)
                    if f > 0:
                        lo(layer, n, f - 1)
                    elif prev:
                        lo(layer, n - 1, FC - 1)
                    if f == 0 and ahead:
                        stats(*ahead)
                    if f == 1 and prev:
                        residual(layer, n - 1)
                    if f == 1 and ahead:
                        center(*ahead)
                    if f == 3 and ahead:
                        ln_lo(*ahead)
                    if f == 4 and behind:
                        wait_alone(ve, s["x_done"], SUB * n)
                        stats(*behind)
                    if f == 5 and behind:
                        center(*behind)
                    if f == 7 and behind:
                        ln_lo(*behind)

            ve.wait_ge(xin[0], 16)
            stats(0, 0)
            ve.wait_ge(ffn_raw, 48)
            for i, r in enumerate((RU, RG, RD)):
                ve.tensor_reduce(PSUMS[:, i:i + 1], r, AX.X, ALU.add, apply_absolute_value=True).then_inc(f_part, 1)
            ve.wait_ge(consts, 6)
            center(0, 0)
            ve.wait_ge(f_tot, 1)
            ve.tensor_scalar(FSC[:, 0:3], FSC[:, 0:3], 1.0 / (D * E), 1e-8, ALU.mult, ALU.add).then_inc(f_sc, 1)
            ve.wait_ge(f_sc, 1)
            ve.tensor_scalar(SU16[:, :], FSC[:, 0:1], 1.0 / LNS, None, ALU.mult)
            ve.tensor_tensor(CY0[:, :], FSC[:, 0:1], FSC[:, 1:2], ALU.mult)
            ve.tensor_scalar(FHALF[:, 0:3], FSC[:, 0:3], 0.5, None, ALU.mult)
            ve.tensor_scalar(FNEG[:, 0:3], FSC[:, 0:3], -0.5, None, ALU.mult)
            ve.reciprocal(FREC[:, 0:1], FSC[:, 0:1]).then_inc(f_sc, 1)
            ve.wait_ge(f_sc, 2)
            ve.tensor_tensor(CY[:, :], CY0[:, :], FSC[:, 2:3], ALU.mult)
            ve.tensor_scalar(CS[:, :], FREC[:, 0:1], HSC, None, ALU.mult).then_inc(f_sc, 1)
            ve.wait_ge(f_sc, 3)
            for i, (r, t) in enumerate(((RU, TU), (RG, TG), (RD, TD))):
                cmp = SCR[:, 0:2048]
                wait(ve, tern, i)
                ve.tensor_scalar(cmp, r, FNEG[:, i:i + 1], None, ALU.is_lt).then_inc(tern_a, 1)
                ve.wait_ge(tern_a, i + 1)
                ve.scalar_tensor_tensor(t[:, :, :].rearrange("p c n -> p (c n)"), r, FHALF[:, i:i + 1], cmp,
                                        ALU.is_gt, ALU.subtract).then_inc(tern, 1)
            ln_lo(0, 0)

            ve.wait_ge(tern, 3)
            ve.wait_ge(xin[1], 16)
            ffn(0, 0, ln_jobs(0), False)
            ve.wait_ge(hs_in, 16)
            ve.wait_ge(attn_raw, 64)
            for h in range(HEADS):
                ve.tensor_scalar(RO[:, h * D:(h + 1) * D], RO[:, h * D:(h + 1) * D], HS[:, h:h + 1], None, ALU.mult).then_inc(hs_mul, 1)
            for i, r in enumerate((RQ, RK, RV, RO)):
                if i == 3:
                    ve.wait_ge(hs_mul, HEADS)
                ve.tensor_reduce(PMAX[:, i:i + 1], r, AX.X, ALU.max, apply_absolute_value=True).then_inc(a_part, 1)
            ve.wait_ge(a_tot, 1)
            ve.tensor_scalar(AMG[:, :], AMAX[:, :], 1e-18, None, ALU.max).then_inc(a_sc_dve, 1)
            ve.wait_ge(a_sc_dve, 1)
            ve.reciprocal(AREC[:, :], AMG[:, :]).then_inc(a_sc_dve, 1)
            ve.tensor_tensor(SCQ0[:, :], AMG[:, 0:1], AMG[:, 1:2], ALU.mult).then_inc(a_sc_dve, 1)
            ve.tensor_tensor(CW0[:, :], AMG[:, 2:3], AMG[:, 3:4], ALU.mult).then_inc(a_sc_dve, 1)
            ve.wait_ge(a_sc_dve, 4)
            ve.tensor_scalar(SCQ[:, :], SCQ0[:, :], DH ** -0.5 / (WTOP * LNS) ** 2, None, ALU.mult)
            ve.tensor_scalar(CW[:, :], CW0[:, :], 1.0 / (VS * WTOP * LNS * WTOP), None, ALU.mult)
            ve.tensor_scalar(AFAC[:, :], AREC[:, :], WTOP, None, ALU.mult).then_inc(a_sc, 1)
            ve.wait_ge(xin[2], 16)
            with ve.Fori(1, TILES - 1) as n:
                ffn(0, n, ln_jobs(n), True)
            ffn(0, TILES - 1, ln_jobs(TILES - 1), True)
            lo(0, TILES - 1, FC - 1)
            residual(0, TILES - 1)
            ve.wait_ge(ff[0]["x_done"], SUB * TILES)
            stats(2 * TILES - 1, TILES - 1)
            center(2 * TILES - 1, TILES - 1)
            ln_lo(2 * TILES - 1, TILES - 1)

            ve.wait_ge(tab_in, 32)
            rpar = [0]

            def rope_mul(r, bk, scaled):
                m = rpar[0]
                rpar[0] ^= 1
                wait(ve, add, r - 1)
                two = lambda a: a.rearrange("p (h n) -> p h n", h=2)
                tab = lambda a, p0, p1: a[p0:p1, :].unsqueeze(1).to_broadcast([p1 - p0, 2, SEQ])
                for dst, d0, d1, s0, s1, tb in ((M1, 0, 128, 0, 128, COS), (M2, 0, 64, 64, 128, SIN), (M2, 64, 128, 0, 64, SIN)):
                    src = two(bk[s0:s1, :])
                    o = two(dst[d0:d1, m, :])
                    if scaled:
                        last = ve.scalar_tensor_tensor(o, src, SCQ[s0:s1, 0:1], tab(tb, s0, s1), ALU.mult, ALU.mult)
                    else:
                        last = ve.tensor_tensor(o, src, tab(tb, s0, s1), ALU.mult)
                last.then_inc(mul, 1)

            def batch(b):
                rpar[0] = 0
                for i in range(PAIRS):
                    g, k = divmod(i, 4)
                    u, t = 2 * b + g, PAIRS * b + i
                    if real(b, i, 1):
                        e, par = t - 1, (i - 1) % 2
                        for hh in range(2):
                            ve.wait_ge(s_done, 2 * e + hh + 1)
                            ve.tensor_reduce(NM[:, par, 2 * hh:2 * hh + 1], SBK[hh][:, 0:128], AX.X, ALU.max, negate=True)
                            ve.tensor_reduce(NM[:, par, 2 * hh + 1:2 * hh + 2], SBK[hh][:, 128:384], AX.X, ALU.max,
                                             negate=True).then_inc(mx, 1)
                    if real(b, i, 0):
                        if k == 0:
                            ve.wait_ge(proj, 6 * u + 1)
                            rope_mul(5 * u, PJ[0], False)
                        ve.wait_ge(proj, 6 * u + (2, 3, 4, 6)[k])
                        rope_mul(5 * u + 1 + k, PJ[(1, 0, 1, 1)[k]], True)
                    if real(b, i, 1):
                        ve.wait_ge(ex, 2 * e + 2)
                        wait(ve, pn, 2 * e - 2)
                        ve.reciprocal(RI[:, par, :], RS[:, par, :]).then_inc(rcp, 1)
                    if real(b, i, 3):
                        e = t - 3
                        ve.wait_ge(oh, e + 1)
                        slot = ((b * PAIRS + i - 3) // PAIRS) % 2 if isinstance(b, int) else ((b + (1 if i >= 3 else 0) + 1) % 2)
                        dst = bass.ds(slot * 4096 + 2 * ((i - 3) % PAIRS) * 256, 512)
                        ve.tensor_tensor(OL[:, dst], OB[:, :], OH[:, dst], ALU.subtract).then_inc(ol, 1)
                    rows_post(b, u, k)

            def rows_post(b, u, k):
                w = post(u)
                if w is None:
                    return
                rows = X[:, bass.ds(w * D, D)]
                if k == 0:
                    ve.wait_ge(w_done, w + 1)
                    ve.scalar_tensor_tensor(rows, WB[:, 0:256], CW[:, 0:1], rows, ALU.mult, ALU.add).then_inc(x2, 1)
                    wait_alone(ve, x2, w + 1)
                    ve.bn_stats(ST[:, 0, :], rows).then_inc(a_st, 1)
                    wait_alone(ve, a_st, w + 1)
                    ve.bn_aggr(MV[:, 0, :], ST[:, 0, :]).then_inc(a_mv, 1)
                if k == 1:
                    ve.wait_ge(a_rs, w + 1)
                    ve.tensor_scalar(XN2, rows, MV[:, 0, 0:1], RSTD[:, 0:1], ALU.subtract, ALU.mult).then_inc(a_xn, 1)
                if k == 2:
                    for c in range(DC):
                        cols = bass.ds(w * P, P)
                        ve.wait_ge(a_xh, 2 * w + c + 1)
                        ve.tensor_tensor(XL[:, c, cols], TB[c][:, 384:512], XH[:, c, cols], ALU.subtract).then_inc(a_xl, 1)

            batches(ve, batch)
            for k in range(3):
                rows_post(BATCH + 1, 2 * BATCH + 2, k)

            ffn(1, 0, (None, None), False)
            with ve.Fori(1, TILES) as n:
                ffn(1, n, (None, None), True)
            lo(1, TILES - 1, FC - 1)
            residual(1, TILES - 1)


def rotary_tables():
    inv = (1.0 / np.float32(10000.0) ** (np.arange(0, DH, 2, dtype=np.float32) / np.float32(DH))).astype(np.float32)
    ang = (np.arange(SEQ, dtype=np.float32)[None, :] * inv[:, None]).astype(np.float32)
    c, s = np.cos(ang), np.sin(ang)
    return np.concatenate([c, c]).astype(np.float32), np.concatenate([s, -s]).astype(np.float32)


def kernel(**inputs):
    import concourse.bacc as bacc
    from concourse.bass_utils import run_bass_kernel_spmd as run

    nc = bacc.Bacc("TRN2", target_bir_lowering=False, num_devices=1)
    cos_t, sin_t = rotary_tables()
    get = lambda n: np.asarray(inputs[n])
    data = {
        "x": get("L0_attn_x"), "wq": get("L0_attn_Wq"), "wk": get("L0_attn_Wk"), "wv": get("L0_attn_Wv"),
        "wo": get("L0_attn_Wo"), "hscale": np.broadcast_to(get("L0_attn_head_scale").reshape(1, HEADS), (P, HEADS)),
        "wu": get("L0_ffn_W_up").T, "wg": get("L0_ffn_W_gate").T, "wd": get("L0_ffn_W_down").T,
        "cos_t": cos_t, "sin_t": sin_t,
    }
    arrays, args = {}, []
    for name, a in data.items():
        arrays["in_" + name] = np.ascontiguousarray(a)
        args.append(nc.dram_tensor("in_" + name, a.shape, mybir.dt.from_np(a.dtype), kind="ExternalInput").ap())
    args.append(nc.dram_tensor("out", (BATCH, SEQ, D), F32, kind="ExternalOutput").ap())
    program(nc, *args)
    return run(nc, [arrays], core_ids=[0]).results[0]["out"]
```

```python
from contextlib import ExitStack

import numpy as np

import concourse.bass as bass
from concourse import mybir

F32 = mybir.dt.float32
F16 = mybir.dt.float16
BF16 = mybir.dt.bfloat16
ALU = mybir.AluOpType
ACT = mybir.ActivationFunctionType
AX = mybir.AxisListType

BATCH, SEQ, D = 16, 256, 256
HEADS, KV, DH = 16, 4, 128
E = 1024
TOK = BATCH * SEQ
P = 128
DC = D // P
FC = E // P
TILE = 512
TILES = TOK // TILE
SUB = TILE // P
PAIRS = HEADS // 2
UNITS = 2 * BATCH
STEPS = BATCH * PAIRS
EPS = 1e-5
LNS = 16.0
WTOP = 1024.0
QS = 2.0 ** -7
VS = 2.0 ** -8
PS = 2.0 ** 12
HSC = 2.0 ** -5
MASKED = -1e36


def program(nc, x, wq, wk, wv, wo, hscale, wu, wg, wd, cos_t, sin_t, out):
    ctx = ExitStack()
    with ctx:
        def sb(name, shape, dt):
            return ctx.enter_context(nc.sbuf_tensor(name, shape, dt))

        def pb(name):
            return ctx.enter_context(nc.psum_tensor(name, [P, 512], F32))

        def sem(name):
            return ctx.enter_context(nc.semaphore(name))

        X = sb("X", [P, TOK // P * D], F32)
        XH = sb("XH", [P, DC, TOK], F16)
        XL = sb("XL", [P, DC, TOK], F16)
        TU = sb("TU", [P, DC, E], F16)
        TG = sb("TG", [P, DC, E], F16)
        TD = sb("TD", [P, FC, D], F16)
        WQH, WQL = (sb(n, [P, DC, HEADS * DH], F16) for n in ("WQH", "WQL"))
        WKH, WKL = (sb(n, [P, DC, KV * DH], F16) for n in ("WKH", "WKL"))
        WVH, WVL = (sb(n, [P, DC, KV * DH], F16) for n in ("WVH", "WVL"))
        WOH, WOL = (sb(n, [P, HEADS, D], F16) for n in ("WOH", "WOL"))
        ARENA = sb("ARENA", [P, 8192], F32)
        RQ, RO = ARENA[:, 0:4096], ARENA[:, 4096:8192]
        OH = ARENA[:, 0:2048].bitcast(F16)
        OL = ARENA[:, 2048:4096].bitcast(F16)
        IDF = sb("IDF", [P, P], F32)
        MASK = sb("MASK", [P, 2 * P], F32)
        SCR = sb("SCR", [P, 9216], F32)
        RU, RG, RD = (SCR[:, i * 2048:(i + 1) * 2048] for i in range(3))
        RK, RV = SCR[:, 7168:8192], SCR[:, 8192:9216]

        def pieces(lo, hi, dt, b):
            a = SCR[:, lo:hi]
            return (a.bitcast(dt) if dt is not F32 else a).rearrange("p (b n) -> p b n", b=b)

        SG, H32 = pieces(0, 1024, F32, 2), pieces(1024, 2048, F32, 2)
        HH, HL = pieces(2048, 3072, F16, 4), pieces(3072, 4096, F16, 4)
        XN = pieces(6144, 7168, F32, 4)
        M1, M2, QK = pieces(0, 1024, F32, 2), pieces(1024, 2048, F32, 2), pieces(2048, 3072, F32, 2)
        QH, QL = pieces(3072, 3584, F16, 2), pieces(3584, 4096, F16, 2)
        KH, KL = pieces(4096, 4608, F16, 2), pieces(4608, 5120, F16, 2)
        VH, VL = pieces(5120, 5376, F16, 2), pieces(5376, 5632, F16, 2)
        EX = SCR[:, 5632:7168].rearrange("p (b h n) -> p b h n", b=2, h=2)
        PH = SCR[:, 7168:7936].bitcast(F16).rearrange("p (b h n) -> p b h n", b=2, h=2)
        PL = SCR[:, 7936:8704].bitcast(F16).rearrange("p (b h n) -> p b h n", b=2, h=2)
        XN2 = pieces(8704, 9216, F32, 2)
        COS = sb("COS", [P, 256], F32)
        SIN = sb("SIN", [P, 256], F32)
        ST = sb("ST", [P, 4, 6], F32)
        MV = sb("MV", [P, 4, 2], F32)
        VE = sb("VE", [P, 4], F32)
        RSTD = sb("RSTD", [P, 4], F32)
        NEGHALF = sb("NEGHALF", [P, 4], F32)
        HS = sb("HS", [P, HEADS], F32)
        PSUMS = sb("PSUMS", [P, 4], F32)
        FSC = sb("FSC", [P, 4], F32)
        FHALF = sb("FHALF", [P, 4], F32)
        FNEG = sb("FNEG", [P, 4], F32)
        FREC = sb("FREC", [P, 4], F32)
        SU16 = sb("SU16", [P, 1], F32)
        CS = sb("CS", [P, 1], F32)
        CY0 = sb("CY0", [P, 1], F32)
        CY = sb("CY", [P, 1], F32)
        PMAX = sb("PMAX", [P, 8], F32)
        AMAX = sb("AMAX", [P, 8], F32)
        AM4 = sb("AM4", [P, 4], F32)
        AMG = sb("AMG", [P, 4], F32)
        AREC = sb("AREC", [P, 4], F32)
        AFAC = sb("AFAC", [P, 4], F32)
        SCQ0 = sb("SCQ0", [P, 1], F32)
        SCQ = sb("SCQ", [P, 1], F32)
        CW0 = sb("CW0", [P, 1], F32)
        CW = sb("CW", [P, 1], F32)
        NM = sb("NM", [P, 2, 4], F32)
        RS = sb("RS", [P, 2, 4], F32)
        RI = sb("RI", [P, 2, 4], F32)

        bank = [pb(f"bank{i}") for i in range(8)]
        UB, GB, YB, TB = bank[0:2], bank[2:4], bank[4:6], bank[6:8]
        PJ, SBK, OB, WB = bank[0:2], bank[2:4], bank[4], bank[5]

        xin = [sem(f"x_in{i}") for i in range(3)]
        ffn_raw = [sem(f"ffn_raw{i}") for i in range(3)]
        attn_raw, hs_in, tab_in = sem("attn_raw"), sem("hs_in"), sem("tab_in")
        consts = sem("consts_ready")
        neghalf = sem("neghalf_ready")
        f_part_act = sem("f_partial_gate")
        f_part, f_tot, f_sc, tern_a, tern = (sem(n) for n in ("f_partial", "f_total", "f_scales", "tern_cmp", "ternary_ready"))
        a_sc_dve = sem("a_scale_steps")
        hs_mul, a_part, a_tot, a_sc = sem("wo_head_scaled"), sem("a_partial"), sem("a_total"), sem("a_scales")
        w_hi, w_ready = sem("w_hi"), sem("attn_weights_ready")
        ln_st, ln_mv, ln_ve, ln_rs, ln_xn, ln_t, ln_xh, ln_xl = (
            sem("ln_" + n) for n in ("stats", "meanvar", "vareps", "rstd", "xn", "turned", "xh", "xl"))
        ff = [{n: sem(f"{n}_{l}") for n in ("u_done", "g_done", "silu_done", "h_done", "hh_done", "hl_done",
                                            "down_done", "y_done", "x_done")} for l in range(2)]
        out_done = sem("out_done")
        proj, swap, mul, add, qk_hi, qk_lo, v_hi, v_lo = (
            sem(n) for n in ("proj_done", "rope_swapped", "rope_mul", "rope_add", "qk_hi", "qk_lo", "v_hi", "v_lo"))
        s_done, mx, ex, rcp, pn = (
            sem(n) for n in ("scores_done", "max_done", "exp_done", "recip_done", "probs_normed"))
        pt_t, p_hi, p_lo, o_done, oh, ol = (
            sem(n) for n in ("probs_turned", "probs_hi", "probs_lo", "o_done", "o_hi", "o_lo"))
        w_done, x2, a_st, a_mv, a_ve, a_rs, a_xn, a_xh, a_xl = (
            sem("at_" + n) for n in ("wo_done", "x2", "stats", "meanvar", "vareps", "rstd", "xn", "xh", "xl"))

        xv = x.rearrange("b (t p) d -> p (b t) d", p=P)
        ov = out.rearrange("b (t p) d -> p (b t) d", p=P)
        XV = X[:, :].rearrange("p (j d) -> p j d", d=D)

        def wait(eng, s, value):
            if not isinstance(value, int) or value > 0:
                eng.wait_ge(s, value)

        def wait_alone(eng, s, value):
            if not isinstance(value, int):
                value = eng.to_reg(value)
                eng.wait_ge(consts, 4)
            eng.wait_ge(s, value)

        BLOCKS = ((0, 128), (128, 384))
        flat = lambda a: a[:, :, :].rearrange("p c n -> p (c n)")
        CUTS = [(RK, WKH, WKL, 0, 1), (RV, WVH, WVL, 0, 2)] + [(RQ, WQH, WQL, o, 0) for o in range(0, 4096, 1024)]
        CUTS += [(RO, WOH, WOL, o, 3) for o in range(0, 4096, 1024)]

        def real(b, i, lag):
            return not isinstance(b, int) or 0 <= PAIRS * b + i - lag < STEPS

        def ln_jobs(n):
            if isinstance(n, int) and n == 0:
                return (1, 1), None
            if isinstance(n, int) and n == TILES - 1:
                return None, (2 * n, n - 1)
            return (2 * n, n + 1), (2 * n + 1, n - 1)

        def ends(b):
            return None if isinstance(b, int) and not 0 <= b - 2 < BATCH else b - 2

        def batches(eng, body):
            body(0)
            body(1)
            with eng.Fori(2, BATCH) as b:
                body(b)
            body(BATCH)

        def turned_rows(j):
            return 2 * STEPS + 2 * j

        def for_tiles(eng, body):
            body(0)
            with eng.Fori(1, TILES) as n:
                body(n)

        block = ctx.enter_context(nc.Block())

        @block.sync
        def _(sp):
            sp.dma_start(RU, wu.rearrange("(c p) e -> p c e", p=P)).then_inc(ffn_raw[0], 16)
            sp.dma_start(RG, wg.rearrange("(c p) e -> p c e", p=P)).then_inc(ffn_raw[1], 16)
            sp.dma_start(RD, wd.rearrange("(c p) d -> p c d", p=P)).then_inc(ffn_raw[2], 16)
            sp.dma_start(XV[:, 4:8, :], xv[:, 4:8, :]).then_inc(xin[1], 16)
            sp.dma_start(RO, wo.rearrange("(h p) d -> p h d", p=P)).then_inc(attn_raw, 16)
            sp.dma_start(RK, wk.rearrange("(c p) e -> p c e", p=P)).then_inc(attn_raw, 16)
            sp.dma_start(RV, wv.rearrange("(c p) e -> p c e", p=P)).then_inc(attn_raw, 16)
            sp.dma_start(RQ, wq.rearrange("(c p) e -> p c e", p=P)).then_inc(attn_raw, 16)
            sp.dma_start(XV[:, 8:32, :], xv[:, 8:32, :]).then_inc(xin[2], 16)
            with sp.Fori(0, TILES) as n:
                sp.wait_ge(ff[1]["x_done"], n * SUB + SUB)
                sp.dma_start(ov[:, bass.ds(n * SUB, SUB), :], XV[:, bass.ds(n * SUB, SUB), :]).then_inc(out_done, 16)
            sp.wait_ge(out_done, 16 * TILES)

        @block.gpsimd
        def _(gp):
            gp.memset(NEGHALF[:, :], -0.5).then_inc(neghalf, 1)
            gp.memset(IDF[:, :], 0.0).then_inc(consts, 1)
            gp.memset(MASK[:, :], 0.0).then_inc(consts, 1)
            gp.wait_ge(consts, 2)
            gp.affine_select(out=IDF[:, :], in_=IDF[:, :], compare_op=ALU.not_equal, fill=1.0, base=0,
                             pattern=[[-1, P]], channel_multiplier=1).then_inc(consts, 1)
            gp.affine_select(out=MASK[:, P:2 * P], in_=MASK[:, P:2 * P], compare_op=ALU.is_ge, fill=MASKED, base=0,
                             pattern=[[-1, P]], channel_multiplier=1).then_inc(consts, 1)
            gp.wait_ge(f_part, 2)
            gp.wait_ge(f_part_act, 1)
            gp.partition_all_reduce(FSC[:, 0:3], PSUMS[:, 0:3], P, bass.bass_isa.ReduceOp.add).then_inc(f_tot, 1)

            def rstd(q):
                wait(gp, ln_xn, 4 * q)
                wait_alone(gp, ln_mv, 4 * q + 4)
                gp.tensor_scalar(VE[:, :], MV[:, :, 1], 1.0 / LNS ** 2, EPS / LNS ** 2, ALU.mult, ALU.add).then_inc(ln_ve, 1)
                gp.wait_ge(ln_ve, q + 1)
                gp.tensor_tensor(RSTD[:, :], VE[:, :], NEGHALF[:, :], ALU.pow).then_inc(ln_rs, 1)

            def ffn(layer, n, jobs):
                s = ff[layer]
                for f in range(FC):
                    gp.wait_ge(s["hh_done"], FC * n + f + 1)
                    gp.tensor_tensor(HL[:, f % 4, :], H32[:, f % 2, :], HH[:, f % 4, :], ALU.subtract).then_inc(s["hl_done"], 1)
                    if f in (0, 4) and jobs[f // 4]:
                        rstd(jobs[f // 4][0])
                    if layer == 1 and isinstance(n, int) and n == 0 and f == 0:
                        rows_rstd(BATCH - 1)

            def rope_add(r, m):
                wait(gp, qk_lo, r - 1)
                gp.wait_ge(mul, r + 1)
                gp.tensor_tensor(QK[:, m, :], M1[:, m, :], M2[:, m, :], ALU.add).then_inc(add, 1)

            def rope_lo(r, m, hi, lo):
                gp.wait_ge(qk_hi, r + 1)
                gp.tensor_tensor(lo, QK[:, m, :], hi, ALU.subtract).then_inc(qk_lo, 1)

            def rows_rstd(e):
                wait_alone(gp, a_mv, 2 * e + 2)
                gp.tensor_scalar(VE[:, 0:2], MV[:, 0:2, 1], 1.0 / LNS ** 2, EPS / LNS ** 2, ALU.mult, ALU.add).then_inc(a_ve, 1)
                gp.wait_ge(a_ve, e + 1)
                gp.tensor_tensor(RSTD[:, 0:2], VE[:, 0:2], NEGHALF[:, 0:2], ALU.pow).then_inc(a_rs, 1)

            def norm(e, par):
                wait_alone(gp, rcp, e + 1)
                for hh in range(2):
                    for blk, (lo, hi) in enumerate(BLOCKS):
                        c = 2 * hh + blk
                        last = gp.tensor_scalar(EX[:, par, hh, lo:hi], EX[:, par, hh, lo:hi], RI[:, par, c:c + 1], PS, ALU.mult, ALU.mult)
                    last.then_inc(pn, 1)

            def batch(b):
                for i in range(PAIRS):
                    g, k = divmod(i, 4)
                    u, t = 2 * b + g, PAIRS * b + i
                    r, m = 5 * u + 1 + k, (5 * g + 1 + k) % 2
                    if real(b, i, 0):
                        if k == 0:
                            rope_add(r - 1, 1 - m)
                        rope_add(r, m)
                    if real(b, i, 2):
                        norm(t - 2, i % 2)
                    if real(b, i, 0):
                        if k == 0:
                            rope_lo(r - 1, 1 - m, KH[:, g, :], KL[:, g, :])
                        rope_lo(r, m, QH[:, i % 2, :], QL[:, i % 2, :])
                    if i == 0 and ends(b) is not None:
                        rows_rstd(ends(b))

            gp.wait_ge(neghalf, 1)
            rstd(0)
            ffn(0, 0, ln_jobs(0))
            gp.wait_ge(a_part, 6)
            gp.partition_all_reduce(AMAX[:, 0:6], PMAX[:, 0:6], P, bass.bass_isa.ReduceOp.max).then_inc(a_tot, 1)
            ffn(0, 1, ln_jobs(1))
            with gp.Fori(2, TILES - 1) as n:
                ffn(0, n, ln_jobs(n))
            ffn(0, TILES - 1, ln_jobs(TILES - 1))
            rstd(2 * TILES - 1)
            batches(gp, batch)
            for_tiles(gp, lambda n: ffn(1, n, (None, None)))

        @block.scalar
        def _(act):
            act.dma_start(XV[:, 0:4, :], xv[:, 0:4, :]).then_inc(xin[0], 16)
            act.dma_start(HS[:, :], hscale).then_inc(hs_in, 16)
            act.dma_start(COS[:, :], cos_t).then_inc(tab_in, 16)
            act.dma_start(SIN[:, :], sin_t).then_inc(tab_in, 16)

            def ln_hi(q, tile):
                for c in range(DC):
                    act.wait_ge(ln_t, 2 * q + c + 1)
                    act.copy(XH[:, c, bass.ds(tile * TILE, TILE)], TB[c][:, :]).then_inc(ln_xh, 1)

            def ffn(layer, n, jobs):
                s = ff[layer]
                for f in range(FC):
                    j = FC * n + f
                    act.wait_ge(s["u_done"], j + 1)
                    wait(act, s["h_done"], j - 1)
                    act.activation(SG[:, f % 2, :], UB[f % 2][:, :], ACT.Silu, scale=SU16[:, 0:1]).then_inc(s["silu_done"], 1)
                    act.wait_ge(s["h_done"], j + 1)
                    wait(act, s["down_done"], j - 3)
                    act.copy(HH[:, f % 4, :], H32[:, f % 2, :]).then_inc(s["hh_done"], 1)
                    if f in (3, 6) and jobs[f // 6]:
                        ln_hi(*jobs[f // 6])
                    if layer == 0 and isinstance(n, int):
                        weights(n, f)
                    if layer == 1 and isinstance(n, int) and n == 0 and f in (3, 5):
                        j = (f - 3) // 2
                        for c in range(DC):
                            act.wait_ge(pt_t, turned_rows(1 + j) + c + 1)
                            rows_hi(BATCH - 1, j, c)

            def weights(n, f):
                if n == 0 and f < 4:
                    if f == 0:
                        act.wait_ge(hs_in, 16)
                        act.wait_ge(attn_raw, 64)
                    for h in range(4 * f, 4 * f + 4):
                        act.mul(RO[:, h * D:(h + 1) * D], RO[:, h * D:(h + 1) * D], HS[:, h:h + 1]).then_inc(hs_mul, 1)
                cut = f - 1 if n == 1 else f + 6 if n == TILES - 1 else -1
                if (0 <= cut < 6 and n == 1) or (6 <= cut < 10):
                    act.wait_ge(a_sc, 1)
                    raw, hi, _, o, c = CUTS[cut]
                    act.mul(flat(hi)[:, o:o + 1024], raw[:, o:o + 1024], AFAC[:, c:c + 1]).then_inc(w_hi, 1)

            def rows_hi(e, j, c):
                act.copy(XH[:, c, bass.ds(e * SEQ + j * P, P)], TB[c][:, 384:512]).then_inc(a_xh, 1)

            act.wait_ge(ffn_raw[1], 16)
            act.activation(flat(TG), RG, ACT.Abs, accum_out=PSUMS[:, 1:2]).then_inc(f_part_act, 1)
            ln_hi(0, 0)
            act.wait_ge(f_sc, 3)
            ffn(0, 0, ln_jobs(0))
            ffn(0, 1, ln_jobs(1))
            with act.Fori(2, TILES - 1) as n:
                ffn(0, n, ln_jobs(n))
            ffn(0, TILES - 1, ln_jobs(TILES - 1))

            def rope_swap(r, m, bk):
                wait(act, add, r - 1)
                for d, s in ((0, 64), (64, 0)):
                    last = act.copy(M2[d:d + 64, m, :], bk[s:s + 64, :])
                last.then_inc(swap, 1)

            def batch(b):
                for i in range(PAIRS):
                    g, k = divmod(i, 4)
                    u, t = 2 * b + g, PAIRS * b + i
                    if real(b, i, 0):
                        r, m = 5 * u + 1 + k, (5 * g + 1 + k) % 2
                        if k == 0:
                            act.wait_ge(proj, 6 * u + 1)
                            rope_swap(r - 1, 1 - m, PJ[0])
                        act.wait_ge(proj, 6 * u + 2 + k)
                        rope_swap(r, m, PJ[(k + 1) % 2])
                    if real(b, i, 2):
                        e, par = t - 2, i % 2
                        wait(act, pt_t, 2 * e - 2)
                        for hh in range(2):
                            act.wait_ge(mx, 2 * e + hh + 1)
                            for blk, (lo, hi) in enumerate(BLOCKS):
                                c = 2 * hh + blk
                                last = act.activation(EX[:, par, hh, lo:hi], SBK[hh][:, lo:hi], ACT.Exp, bias=NM[:, par, c:c + 1],
                                                      scale=-1.0, accum_out=RS[:, par, c:c + 1])
                            last.then_inc(ex, 1)
                    if real(b, i, 4):
                        e = t - 4
                        act.wait_ge(o_done, e + 1)
                        h = 2 * ((i - 4) % PAIRS) * SEQ
                        act.mul(OH[:, h:h + 2 * SEQ], OB[:, :], 1.0 / PS).then_inc(oh, 1)
                    if k == 3 and real(b, i, 0):
                        act.wait_ge(proj, 6 * u + 6)
                        wait(act, o_done, 4 * u)
                        act.mul(VH[:, :, :].rearrange("p j n -> p (j n)"), PJ[1][:, :], VS).then_inc(v_hi, 1)
                    if isinstance(b, int) and b + i == 0:
                        ln_hi(2 * TILES - 1, TILES - 1)
                    rows = i in (2, 3) and ends(b) is not None
                    for hh in range(2):
                        if real(b, i, 3):
                            e = t - 3
                            act.wait_ge(pt_t, 2 * e + hh + 1)
                            wait(act, o_done, e - 1)
                            act.copy(PH[:, (i - 3) % 2, hh, :], TB[hh][:, 0:384]).then_inc(p_hi, 1)
                        elif rows:
                            act.wait_ge(pt_t, turned_rows(0) + hh + 1)
                        if rows:
                            rows_hi(ends(b), i - 2, hh)
                    if real(b, i, 0):
                        if k == 0:
                            act.wait_ge(add, r)
                            wait(act, s_done, 8 * u - 8)
                            act.copy(KH[:, g, :], QK[:, 1 - m, :]).then_inc(qk_hi, 1)
                        act.wait_ge(add, r + 1)
                        wait(act, s_done, 2 * t - 2)
                        act.copy(QH[:, i % 2, :], QK[:, m, :]).then_inc(qk_hi, 1)

            batches(act, batch)

            for_tiles(act, lambda n: ffn(1, n, (None, None)))

        @block.tensor
        def _(pe):
            def turn(q):
                wait(pe, ln_xl, 2 * q)
                for s in range(SUB):
                    pe.wait_ge(ln_xn, 4 * q + s + 1)
                    if s == SUB - 1:
                        break
                for c in range(DC):
                    for s in range(SUB):
                        last = pe.transpose(TB[c][:, s * P:(s + 1) * P], XN[:, s, c * P:(c + 1) * P], IDF[:, :])
                    last.then_inc(ln_t, 1)

            def up(layer, n, f):
                s = ff[layer]
                j = FC * n + f
                cols = bass.ds(n * TILE, TILE)
                wait(pe, s["silu_done"], j - 1)
                for a, xs in enumerate((XH, XL)):
                    for c in range(DC):
                        last = pe.matmul(UB[f % 2][:, :], TU[:, c, f * P:(f + 1) * P], xs[:, c, cols],
                                         start=a + c == 0, stop=a + c == 2)
                last.then_inc(s["u_done"], 1)
                wait(pe, s["h_done"], j - 1)
                for a, xs in enumerate((XH, XL)):
                    for c in range(DC):
                        last = pe.matmul(GB[f % 2][:, :], TG[:, c, f * P:(f + 1) * P], xs[:, c, cols],
                                         start=a + c == 0, stop=a + c == 2)
                last.then_inc(s["g_done"], 1)

            def down(layer, n, f):
                s = ff[layer]
                j = FC * n + f
                pe.wait_ge(s["hl_done"], j + 1)
                if f == 0:
                    wait(pe, s["x_done"], SUB * n)
                if f == 0 and isinstance(n, int) and n == 0:
                    pe.wait_ge(*((tern, 3), (x2, UNITS))[layer])
                for sub in range(SUB):
                    for a, hs in enumerate((HH, HL)):
                        last = pe.matmul(YB[sub // 2][:, (sub % 2) * D:(sub % 2 + 1) * D], hs[:, f % 4, sub * P:(sub + 1) * P],
                                         TD[:, f, :], start=f == 0 and a == 0 and sub % 2 == 0,
                                         stop=f == FC - 1 and a == 1, skip_group_check=True)
                last.then_inc(s["down_done"], 1)

            def ffn(layer, n, jobs, prev):
                for f in range(FC):
                    up(layer, n, f)
                    if f >= 2:
                        down(layer, n, f - 2)
                    elif prev:
                        down(layer, n - 1, f + FC - 2)
                    if f in (2, 6) and jobs[f // 6]:
                        turn(jobs[f // 6][0])
                    if layer == 1 and isinstance(n, int) and n == 0 and f in (2, 4):
                        turn_rows(BATCH - 1, (f - 2) // 2)

            pe.wait_ge(consts, 4)
            turn(0)
            pe.wait_ge(tern, 2)
            pe.wait_ge(ln_xl, 2)
            ffn(0, 0, ln_jobs(0), False)
            pe.wait_ge(ln_xl, 4)
            ffn(0, 1, ln_jobs(1), True)
            with pe.Fori(2, TILES - 1) as n:
                pe.wait_ge(ln_xl, 4 * n - 2)
                ffn(0, n, ln_jobs(n), True)
            pe.wait_ge(ln_xl, 4 * TILES - 6)
            ffn(0, TILES - 1, ln_jobs(TILES - 1), True)
            down(0, TILES - 1, FC - 2)
            down(0, TILES - 1, FC - 1)

            def pairs(dst, lh, ll, rh, rl, n, start, stop):
                todo = [(l, r, c) for l, r in ((lh, rh), (lh, rl), (ll, rh)) for c in range(n)]
                for x, (l, r, c) in enumerate(todo):
                    last = pe.matmul(dst, l(c), r(c), start=start and x == 0, stop=stop and x == len(todo) - 1,
                                     skip_group_check=True)
                return last

            def project_qk(dst, wh, wl, h0, b):
                cols = bass.ds(b * SEQ, SEQ)
                for hh in range(2):
                    w = slice((h0 + hh) * DH, (h0 + hh + 1) * DH)
                    last = pairs(dst[:, hh * SEQ:(hh + 1) * SEQ], lambda c: wh[:, c, w], lambda c: wl[:, c, w],
                                 lambda c: XH[:, c, cols], lambda c: XL[:, c, cols], DC, hh == 0, hh == 1)
                last.then_inc(proj, 1)

            def project_v(dst, b, g):
                for j in range(2):
                    rows = bass.ds(b * SEQ + j * P, P)
                    w = slice(g * 256, g * 256 + 256)
                    last = pairs(dst[:, j * 256:(j + 1) * 256], lambda c: XH[:, c, rows], lambda c: XL[:, c, rows],
                                 lambda c: WVH[:, c, w], lambda c: WVL[:, c, w], DC, j == 0, j == 1)
                last.then_inc(proj, 1)

            def scores(t, i, u):
                pe.wait_ge(qk_lo, 5 * u + i % 4 + 2)
                g, kv = i // 4, i % 4 // 2
                for hh in range(2):
                    wait(pe, ex, 2 * t + hh - 1)
                    bk = SBK[hh]
                    for blk, (lo, hi) in enumerate(BLOCKS):
                        q = [a[:, i % 2, hh * SEQ + blk * P:hh * SEQ + (blk + 1) * P] for a in (QH, QL)]
                        k = [a[:, g, kv * SEQ:kv * SEQ + hi - lo] for a in (KH, KL)]
                        last = pairs(bk[:, lo:hi], lambda c: q[0], lambda c: q[1], lambda c: k[0], lambda c: k[1], 1, blk == 0, blk == 1)
                    last.then_inc(s_done, 1)

            def values(t, i, u):
                kv = i % 4 // 2
                pe.wait_ge(v_lo, u + 1)
                wait(pe, ol, t)
                vs = slice(kv * DH, (kv + 1) * DH)
                for hh in range(2):
                    pe.wait_ge(p_lo, 2 * t + hh + 1)
                    ph, pl = PH[:, i % 2, hh, :], PL[:, i % 2, hh, :]
                    o = hh * SEQ
                    pairs(OB[:, o:o + 256], lambda c: VH[:, 0, vs], lambda c: VL[:, 0, vs],
                          lambda c: ph[:, 0:256], lambda c: pl[:, 0:256], 1, hh == 0, False)
                    last = pairs(OB[:, o + 128:o + 256], lambda c: VH[:, 1, vs], lambda c: VL[:, 1, vs],
                                 lambda c: ph[:, 256:384], lambda c: pl[:, 256:384], 1, False, hh == 1)
                last.then_inc(o_done, 1)

            def turn_probs(t, i, e, j):
                for hh in range(2):
                    wait(pe, p_lo, 2 * t + hh - 1)
                    if e is not None and j in (1, 2):
                        pe.wait_ge(a_xl, 4 * e + 2 * j + hh - 1)
                    pe.wait_ge(pn, 2 * t + hh + 1)
                    for blk in range(3):
                        last = pe.transpose(TB[hh][:, blk * P:(blk + 1) * P], EX[:, i % 2, hh, blk * P:(blk + 1) * P], IDF[:, :])
                    if e is not None and j in (0, 1):
                        pe.wait_ge(a_xn, 2 * e + j + 1)
                        last = pe.transpose(TB[hh][:, 384:512], XN2[:, j, hh * P:(hh + 1) * P], IDF[:, :])
                    last.then_inc(pt_t, 1)

            def turn_rows(e, j):
                pe.wait_ge(p_lo, 2 * STEPS)
                pe.wait_ge(a_xl, 4 * e + 2 * j)
                pe.wait_ge(a_xn, 2 * e + j + 1)
                for c in range(DC):
                    pe.transpose(TB[c][:, 384:512], XN2[:, j, c * P:(c + 1) * P], IDF[:, :]).then_inc(pt_t, 1)

            def output(b, i):
                pe.wait_ge(ol, PAIRS * (b - 1) + i + 1)
                if i == 0:
                    wait(pe, x2, 2 * (b - 1))
                for h in (2 * i, 2 * i + 1):
                    for j in range(2):
                        rows = slice(h * SEQ + j * P, h * SEQ + (j + 1) * P)
                        last = pairs(WB[:, j * 256:(j + 1) * 256], lambda c: OH[:, rows], lambda c: OL[:, rows],
                                     lambda c: WOH[:, h, :], lambda c: WOL[:, h, :], 1, h == 0 and j == 0, h == HEADS - 1 and j == 1)
                if i == PAIRS - 1:
                    last.then_inc(w_done, 1)

            def batch(b):
                for i in range(PAIRS):
                    g, k = divmod(i, 4)
                    u, t = 2 * b + g, PAIRS * b + i
                    unit = lambda lag: 2 * b + (i - lag) // 4
                    if real(b, i, 0):
                        if k == 0:
                            wait(pe, mul, 5 * u)
                            project_qk(PJ[0], WKH, WKL, 2 * g, b)
                            wait(pe, v_lo, u)
                        else:
                            pe.wait_ge(mul, 5 * u + k)
                        project_qk(PJ[(k + 1) % 2], WQH, WQL, 8 * g + 2 * k, b)
                    if real(b, i, 2):
                        scores(t - 2, (i - 2) % PAIRS, unit(2))
                    if real(b, i, 4):
                        values(t - 4, (i - 4) % PAIRS, unit(4))
                    if real(b, i, 0) and k == 3:
                        pe.wait_ge(mul, 5 * u + 4)
                        project_v(PJ[1], b, g)
                    if real(b, i, 3):
                        turn_probs(t - 3, (i - 3) % PAIRS, ends(b), i - 2)
                    elif i == 3 and ends(b) is not None:
                        turn_rows(ends(b), 1)
                    if isinstance(b, int) and b + i == 0:
                        turn(2 * TILES - 1)
                    if not isinstance(b, int) or b > 0:
                        output(b, i)

            pe.wait_ge(w_ready, 10)
            batches(pe, batch)

            ffn(1, 0, (None, None), False)
            with pe.Fori(1, TILES) as n:
                ffn(1, n, (None, None), True)
            down(1, TILES - 1, FC - 2)
            down(1, TILES - 1, FC - 1)

        @block.vector
        def _(ve):
            def stats(q, tile):
                for s in range(SUB):
                    ve.bn_stats(ST[:, s, :], X[:, bass.ds(tile * (SUB * D) + s * D, D)]).then_inc(ln_st, 1)
                for s in range(SUB):
                    wait_alone(ve, ln_st, 4 * q + s + 1)
                    ve.bn_aggr(MV[:, s, :], ST[:, s, :]).then_inc(ln_mv, 1)

            def center(q, tile):
                ve.wait_ge(ln_rs, q + 1)
                wait(ve, ln_t, 2 * q)
                for s in range(SUB):
                    ve.tensor_scalar(XN[:, s, :], X[:, bass.ds(tile * (SUB * D) + s * D, D)], MV[:, s, 0:1],
                                     RSTD[:, s:s + 1], ALU.subtract, ALU.mult).then_inc(ln_xn, 1)

            def ln_lo(q, tile):
                for c in range(DC):
                    cols = bass.ds(tile * TILE, TILE)
                    ve.wait_ge(ln_xh, 2 * q + c + 1)
                    ve.tensor_tensor(XL[:, c, cols], TB[c][:, :], XH[:, c, cols], ALU.subtract).then_inc(ln_xl, 1)

            def residual(layer, tile):
                s = ff[layer]
                ve.wait_ge(s["down_done"], FC * tile + FC)
                for sub in range(SUB):
                    rows = X[:, bass.ds(tile * (SUB * D) + sub * D, D)]
                    ve.scalar_tensor_tensor(rows, YB[sub // 2][:, (sub % 2) * D:(sub % 2 + 1) * D], CY[:, 0:1], rows,
                                            ALU.mult, ALU.add).then_inc(s["x_done"], 1)

            def ffn(layer, n, jobs, prev):
                s = ff[layer]
                ahead, behind = jobs
                for f in range(FC):
                    j = FC * n + f
                    ve.wait_ge(s["silu_done"], j + 1)
                    ve.wait_ge(s["g_done"], j + 1)
                    wait(ve, s["hl_done"], j - 1)
                    ve.scalar_tensor_tensor(H32[:, f % 2, :], SG[:, f % 2, :], CS[:, 0:1], GB[f % 2][:, :],
                                            ALU.mult, ALU.mult).then_inc(s["h_done"], 1)
                    if layer == 0 and isinstance(n, int):
                        weights(n, f)
                    if layer == 1 and isinstance(n, int) and n == 0:
                        last_rows(f)
                    if f == 0 and ahead:
                        stats(*ahead)
                    if f == 1 and prev:
                        residual(layer, n - 1)
                    if f == 1 and ahead:
                        center(*ahead)
                    if f == 3 and ahead:
                        ln_lo(*ahead)
                    if f == 4 and behind:
                        wait_alone(ve, s["x_done"], SUB * n)
                        stats(*behind)
                    if f == 5 and behind:
                        center(*behind)
                    if f == 7 and behind:
                        ln_lo(*behind)

            def weights(n, f):
                maxima = {2: (RK, 0, 1024, 1), 3: (RV, 0, 1024, 2), 4: (RQ, 0, 2048, 0), 5: (RQ, 2048, 4096, 4),
                          6: (RO, 0, 2048, 3), 7: (RO, 2048, 4096, 5)}
                if n == 0 and f in maxima:
                    raw, a, z, c = maxima[f]
                    if f == 2:
                        ve.wait_ge(attn_raw, 64)
                    if f == 6:
                        ve.wait_ge(hs_mul, HEADS)
                    ve.tensor_reduce(PMAX[:, c:c + 1], raw[:, a:z], AX.X, ALU.max, apply_absolute_value=True).then_inc(a_part, 1)
                if n == 1 and f == 0:
                    scales()
                cut = f - 2 if n == 1 else f + 5 if n == TILES - 1 else -1
                if (0 <= cut < 6 and n == 1) or (6 <= cut < 10):
                    ve.wait_ge(w_hi, cut + 1)
                    raw, hi, lo, o, c = CUTS[cut]
                    ve.scalar_tensor_tensor(flat(lo)[:, o:o + 1024], raw[:, o:o + 1024], AFAC[:, c:c + 1],
                                            flat(hi)[:, o:o + 1024], ALU.mult, ALU.subtract).then_inc(w_ready, 1)

            def scales():
                ve.wait_ge(a_tot, 1)
                ve.tensor_scalar(AM4[:, :], AMAX[:, 0:4], 1e-18, None, ALU.max).then_inc(a_sc_dve, 1)
                ve.wait_ge(a_sc_dve, 1)
                ve.tensor_tensor(AMG[:, 1:3], AM4[:, 1:3], AM4[:, 1:3], ALU.max)
                ve.tensor_tensor(AMG[:, 0:1], AM4[:, 0:1], AMAX[:, 4:5], ALU.max)
                ve.tensor_tensor(AMG[:, 3:4], AM4[:, 3:4], AMAX[:, 5:6], ALU.max).then_inc(a_sc_dve, 1)
                ve.wait_ge(a_sc_dve, 2)
                ve.reciprocal(AREC[:, :], AMG[:, :])
                ve.tensor_tensor(SCQ0[:, :], AMG[:, 0:1], AMG[:, 1:2], ALU.mult)
                ve.tensor_tensor(CW0[:, :], AMG[:, 2:3], AMG[:, 3:4], ALU.mult).then_inc(a_sc_dve, 1)
                ve.wait_ge(a_sc_dve, 3)
                ve.tensor_scalar(SCQ[:, :], SCQ0[:, :], -DH ** -0.5 / (WTOP * LNS * QS) ** 2, None, ALU.mult)
                ve.tensor_scalar(CW[:, :], CW0[:, :], 1.0 / (VS * WTOP * LNS * WTOP), None, ALU.mult)
                ve.tensor_scalar(AFAC[:, :], AREC[:, :], WTOP, None, ALU.mult).then_inc(a_sc, 1)

            ve.wait_ge(ffn_raw[0], 16)
            ve.tensor_reduce(PSUMS[:, 0:1], RU, AX.X, ALU.add, apply_absolute_value=True).then_inc(f_part, 1)
            ve.wait_ge(xin[0], 16)
            stats(0, 0)
            ve.wait_ge(ffn_raw[2], 16)
            ve.tensor_reduce(PSUMS[:, 2:3], RD, AX.X, ALU.add, apply_absolute_value=True).then_inc(f_part, 1)
            ve.wait_ge(consts, 4)
            center(0, 0)
            ve.wait_ge(f_tot, 1)
            ve.tensor_scalar(FSC[:, 0:3], FSC[:, 0:3], 1.0 / (D * E), 1e-8, ALU.mult, ALU.add).then_inc(f_sc, 1)
            ve.wait_ge(f_sc, 1)
            ve.tensor_scalar(SU16[:, :], FSC[:, 0:1], 1.0 / LNS, None, ALU.mult)
            ve.tensor_tensor(CY0[:, :], FSC[:, 0:1], FSC[:, 1:2], ALU.mult)
            ve.tensor_scalar(FHALF[:, 0:3], FSC[:, 0:3], 0.5, None, ALU.mult)
            ve.tensor_scalar(FNEG[:, 0:3], FSC[:, 0:3], -0.5, None, ALU.mult)
            ve.reciprocal(FREC[:, 0:1], FSC[:, 0:1]).then_inc(f_sc, 1)
            ve.wait_ge(f_sc, 2)
            ve.tensor_tensor(CY[:, :], CY0[:, :], FSC[:, 2:3], ALU.mult)
            ve.tensor_scalar(CS[:, :], FREC[:, 0:1], HSC, None, ALU.mult).then_inc(f_sc, 1)
            for i, (r, t) in enumerate(((RU, TU), (RG, TG), (RD, TD))):
                ve.wait_ge(ffn_raw[i], 16)
                if i == 1:
                    ve.wait_ge(f_part_act, 1)
                ve.tensor_scalar(flat(t), r, FNEG[:, i:i + 1], None, ALU.is_lt).then_inc(tern_a, 1)
                ve.wait_ge(tern_a, i + 1)
                ve.scalar_tensor_tensor(flat(t), r, FHALF[:, i:i + 1], flat(t), ALU.is_gt, ALU.subtract).then_inc(tern, 1)
                if i == 0:
                    ln_lo(0, 0)

            ve.wait_ge(xin[1], 16)
            ffn(0, 0, ln_jobs(0), False)
            ve.wait_ge(xin[2], 16)
            ffn(0, 1, ln_jobs(1), True)
            with ve.Fori(2, TILES - 1) as n:
                ffn(0, n, ln_jobs(n), True)
            ffn(0, TILES - 1, ln_jobs(TILES - 1), True)
            residual(0, TILES - 1)

            ve.wait_ge(tab_in, 32)

            def rope_mul(r, m, bk):
                wait(ve, add, r - 1)
                ve.wait_ge(swap, r + 1)
                two = lambda a: a.rearrange("p (h n) -> p h n", h=2)
                for dst, src, tb in ((M1[:, m, :], bk[:, :], COS), (M2[:, m, :], M2[:, m, :], SIN)):
                    last = ve.tensor_tensor(two(dst), two(src), tb[:, :].unsqueeze(1).to_broadcast([P, 2, SEQ]), ALU.mult)
                last.then_inc(mul, 1)

            def batch(b):
                for i in range(PAIRS):
                    g, k = divmod(i, 4)
                    u, t = 2 * b + g, PAIRS * b + i
                    r, m = 5 * u + 1 + k, (5 * g + 1 + k) % 2
                    if i == 0 and ends(b) is not None:
                        rows_residual(ends(b))
                    if k == 0 and real(b, i, 0):
                        rope_mul(r - 1, 1 - m, PJ[0])
                    if real(b, i, 2):
                        e, par = t - 2, i % 2
                        for hh in range(2):
                            wait_alone(ve, s_done, 2 * e + hh + 1)
                            for blk, (lo, hi) in enumerate(BLOCKS):
                                c = 2 * hh + blk
                                last = ve.tensor_tensor_reduce(SBK[hh][:, lo:hi], SBK[hh][:, lo:hi], MASK[:, 256 - (hi - lo):256],
                                                               SCQ[:, 0:1], 3e38, ALU.add, ALU.min, NM[:, par, c:c + 1])
                            last.then_inc(mx, 1)
                    if real(b, i, 0):
                        rope_mul(r, m, PJ[(k + 1) % 2])
                    if isinstance(b, int) and b + i == 0:
                        ve.wait_ge(ff[0]["x_done"], SUB * TILES)
                        stats(2 * TILES - 1, TILES - 1)
                        center(2 * TILES - 1, TILES - 1)
                        ln_lo(2 * TILES - 1, TILES - 1)
                    if real(b, i, 2):
                        ve.wait_ge(ex, 2 * e + 2)
                        wait(ve, pn, 2 * e - 2)
                        ve.reciprocal(RI[:, par, :], RS[:, par, :]).then_inc(rcp, 1)
                    if real(b, i, 4):
                        ve.wait_ge(oh, t - 3)
                        h = 2 * ((i - 4) % PAIRS) * SEQ
                        ve.scalar_tensor_tensor(OL[:, h:h + 2 * SEQ], OB[:, :], 1.0 / PS, OH[:, h:h + 2 * SEQ],
                                                ALU.mult, ALU.subtract).then_inc(ol, 1)
                    if k == 3 and real(b, i, 0):
                        ve.wait_ge(v_hi, u + 1)
                        ve.scalar_tensor_tensor(VL[:, :, :].rearrange("p j n -> p (j n)"), PJ[1][:, :], VS,
                                                VH[:, :, :].rearrange("p j n -> p (j n)"), ALU.mult, ALU.subtract).then_inc(v_lo, 1)
                    if i == 1 and ends(b) is not None:
                        rows_center(ends(b))
                    for hh in range(2):
                        if i in (2, 3) and ends(b) is not None:
                            ve.wait_ge(a_xh, 4 * ends(b) + 2 * (i - 2) + hh + 1)
                        if real(b, i, 3):
                            ve.wait_ge(p_hi, 2 * (t - 3) + hh + 1)
                            par = (i - 3) % 2
                            ve.tensor_tensor(PL[:, par, hh, :], TB[hh][:, 0:384], PH[:, par, hh, :], ALU.subtract).then_inc(p_lo, 1)
                        if i in (2, 3) and ends(b) is not None:
                            rows_lo(ends(b), i - 2, hh)
                    if i == 0 and ends(b) is not None:
                        rows_stats(ends(b))

            def rows_residual(e):
                ve.wait_ge(w_done, e + 1)
                for j in range(2):
                    rows = X[:, bass.ds(e * (2 * D) + j * D, D)]
                    ve.scalar_tensor_tensor(rows, WB[:, j * 256:(j + 1) * 256], CW[:, 0:1], rows, ALU.mult, ALU.add).then_inc(x2, 1)

            def rows_stats(e):
                for j in range(2):
                    wait_alone(ve, x2, 2 * e + j + 1)
                    ve.bn_stats(ST[:, j, :], X[:, bass.ds(e * (2 * D) + j * D, D)]).then_inc(a_st, 1)
                for j in range(2):
                    wait_alone(ve, a_st, 2 * e + j + 1)
                    ve.bn_aggr(MV[:, j, :], ST[:, j, :]).then_inc(a_mv, 1)

            def rows_center(e):
                ve.wait_ge(a_rs, e + 1)
                for j in range(2):
                    ve.tensor_scalar(XN2[:, j, :], X[:, bass.ds(e * (2 * D) + j * D, D)], MV[:, j, 0:1], RSTD[:, j:j + 1],
                                     ALU.subtract, ALU.mult).then_inc(a_xn, 1)

            def rows_lo(e, j, c):
                cols = bass.ds(e * SEQ + j * P, P)
                ve.wait_ge(a_xh, 4 * e + 2 * j + c + 1)
                ve.tensor_tensor(XL[:, c, cols], TB[c][:, 384:512], XH[:, c, cols], ALU.subtract).then_inc(a_xl, 1)

            def last_rows(f):
                if f == 1:
                    rows_center(BATCH - 1)
                if f in (3, 5):
                    for c in range(DC):
                        rows_lo(BATCH - 1, (f - 3) // 2, c)

            batches(ve, batch)
            rows_residual(BATCH - 1)
            rows_stats(BATCH - 1)

            ffn(1, 0, (None, None), False)
            with ve.Fori(1, TILES) as n:
                ffn(1, n, (None, None), True)
            residual(1, TILES - 1)


def rotary_tables():
    inv = (1.0 / np.float32(10000.0) ** (np.arange(0, DH, 2, dtype=np.float32) / np.float32(DH))).astype(np.float32)
    ang = (np.arange(SEQ, dtype=np.float32)[None, :] * inv[:, None]).astype(np.float32)
    c, s = np.cos(ang), np.sin(ang)
    c, s = np.float32(QS) * c.astype(np.float32), np.float32(QS) * s.astype(np.float32)
    return np.concatenate([c, c]), np.concatenate([-s, s])


def kernel(**inputs):
    import concourse.bacc as bacc
    from concourse.bass_utils import run_bass_kernel_spmd as run

    nc = bacc.Bacc("TRN2", target_bir_lowering=False, num_devices=1)
    cos_t, sin_t = rotary_tables()
    get = lambda n: np.asarray(inputs[n])
    data = {
        "x": get("L0_attn_x"), "wq": get("L0_attn_Wq"), "wk": get("L0_attn_Wk"), "wv": get("L0_attn_Wv"),
        "wo": get("L0_attn_Wo"), "hscale": np.broadcast_to(get("L0_attn_head_scale").reshape(1, HEADS), (P, HEADS)),
        "wu": get("L0_ffn_W_up").T, "wg": get("L0_ffn_W_gate").T, "wd": get("L0_ffn_W_down").T,
        "cos_t": cos_t, "sin_t": sin_t,
    }
    arrays, args = {}, []
    for name, a in data.items():
        arrays["in_" + name] = np.ascontiguousarray(a)
        args.append(nc.dram_tensor("in_" + name, a.shape, mybir.dt.from_np(a.dtype), kind="ExternalInput").ap())
    args.append(nc.dram_tensor("out", (BATCH, SEQ, D), F32, kind="ExternalOutput").ap())
    program(nc, *args)
    return run(nc, [arrays], core_ids=[0]).results[0]["out"]
```

```python
from contextlib import ExitStack

import numpy as np

import concourse.bass as bass
from concourse import mybir

F32 = mybir.dt.float32
F16 = mybir.dt.float16
ALU = mybir.AluOpType
ACT = mybir.ActivationFunctionType
AX = mybir.AxisListType

BATCH, SEQ, D = 16, 256, 256
HEADS, KV, DH = 16, 4, 128
E = 1024
TOK = BATCH * SEQ
P = 128
DC = D // P
FC = E // P
TILE = 512
TILES = TOK // TILE
SUB = TILE // P
PAIRS = HEADS // 2
STEPS = BATCH * PAIRS
EPS = 1e-5
LNS = 16.0
WTOP = 1024.0
WMIN = 1e-12
QS = 2.0 ** -7
VS = 2.0 ** -8
PS = 2.0 ** 12
HSC = 2.0 ** -5
MASKED = -1e36


def program(nc, x, wq, wk, wv, wo, hscale, wu, wg, wd, cos_t, sin_t, out):
    ctx = ExitStack()
    with ctx:
        def sb(name, shape, dt):
            return ctx.enter_context(nc.sbuf_tensor(name, shape, dt))

        def pb(name):
            return ctx.enter_context(nc.psum_tensor(name, [P, 512], F32))

        def sem(name):
            return ctx.enter_context(nc.semaphore(name))

        X = sb("X", [P, TOK // P * D], F32)
        XH = sb("XH", [P, DC, TOK], F16)
        XL = sb("XL", [P, DC, TOK], F16)
        TU = sb("TU", [P, DC, E], F16)
        TG = sb("TG", [P, DC, E], F16)
        TD = sb("TD", [P, FC, D], F16)
        WQH, WQL = (sb(n, [P, DC, HEADS * DH], F16) for n in ("WQH", "WQL"))
        WKH, WKL = (sb(n, [P, DC, KV * DH], F16) for n in ("WKH", "WKL"))
        WVH, WVL = (sb(n, [P, DC, KV * DH], F16) for n in ("WVH", "WVL"))
        WOH, WOL = (sb(n, [P, HEADS, D], F16) for n in ("WOH", "WOL"))
        ARENA = sb("ARENA", [P, 8192], F32)
        RQ, RO = ARENA[:, 0:4096], ARENA[:, 4096:8192]
        OH = ARENA[:, 0:2048].bitcast(F16)
        OL = ARENA[:, 2048:4096].bitcast(F16)
        XN7 = ARENA[:, 4096:5120].rearrange("p (b n) -> p b n", b=4)
        IDF = sb("IDF", [P, P], F32)
        MASK = sb("MASK", [P, 2 * P], F32)
        SCR = sb("SCR", [P, 9216], F32)
        RU, RG, RD = X[:, 4096:6144], X[:, 6144:8192], SCR[:, 4096:6144]
        RK, RV = SCR[:, 7168:8192], SCR[:, 8192:9216]

        def pieces(lo, hi, dt, b):
            a = SCR[:, lo:hi]
            return (a.bitcast(dt) if dt is not F32 else a).rearrange("p (b n) -> p b n", b=b)

        SG, H32 = pieces(0, 1024, F32, 2), pieces(1024, 2048, F32, 2)
        HH, HL = pieces(2048, 3072, F16, 4), pieces(3072, 4096, F16, 4)
        XN = pieces(6144, 7168, F32, 4)
        M1, M2, QK = pieces(0, 1024, F32, 2), pieces(1024, 2048, F32, 2), pieces(2048, 3072, F32, 2)
        QH, QL = pieces(3072, 3584, F16, 2), pieces(3584, 4096, F16, 2)
        KH, KL = pieces(4096, 4608, F16, 2), pieces(4608, 5120, F16, 2)
        VH, VL = (ARENA[:, lo:lo + 512].bitcast(F16).rearrange("p (g n) -> p g n", g=2) for lo in (6656, 7168))
        EX = SCR[:, 5632:7168].rearrange("p (b n) -> p b n", b=2)
        PR = ARENA[:, 5120:6656].bitcast(F16).rearrange("p (b n) -> p b n", b=2)
        PT = SCR[:, 7168:8704].bitcast(F16).rearrange("p (b k n) -> p b k n", b=2, k=12)
        XN2 = pieces(8704, 9216, F32, 2)
        COS = sb("COS", [P, 256], F32)
        SIN = sb("SIN", [P, 256], F32)
        ST = sb("ST", [P, 4, 6], F32)
        MV = sb("MV", [P, 4, 2], F32)
        VE = sb("VE", [P, 4], F32)
        RSTD = sb("RSTD", [P, 4], F32)
        NEGHALF = sb("NEGHALF", [P, 4], F32)
        WARM = sb("WARM", [P, 2], F32)
        HS = sb("HS", [P, HEADS], F32)
        PSUMS = sb("PSUMS", [P, 4], F32)
        FTOT = sb("FTOT", [P, 4], F32)
        FSC = sb("FSC", [P, 4], F32)
        FHALF = sb("FHALF", [P, 4], F32)
        FNEG = sb("FNEG", [P, 4], F32)
        FREC = sb("FREC", [P, 4], F32)
        SU16 = sb("SU16", [P, 1], F32)
        CS = sb("CS", [P, 1], F32)
        CY0 = sb("CY0", [P, 1], F32)
        CY = sb("CY", [P, 1], F32)
        PMAX = sb("PMAX", [P, 16], F32)
        PM4 = sb("PM4", [P, 4], F32)
        AMAX = sb("AMAX", [P, 4], F32)
        AMG = sb("AMG", [P, 4], F32)
        AREC = sb("AREC", [P, 4], F32)
        AFAC = sb("AFAC", [P, 4], F32)
        SCQ0 = sb("SCQ0", [P, 1], F32)
        SCQ = sb("SCQ", [P, 1], F32)
        CW0 = sb("CW0", [P, 1], F32)
        CW = sb("CW", [P, 1], F32)
        NM = sb("NM", [P, 2, 4], F32)
        RS = sb("RS", [P, 2, 4], F32)
        RI = sb("RI", [P, 2, 4], F32)

        bank = [pb(f"bank{i}") for i in range(8)]
        UB, GB, YB, TB = bank[0:2], bank[2:4], bank[4:6], bank[6:8]
        PJ, SBK, OB, WB, RB = bank[0:2], bank[2:4], (bank[4], bank[6]), bank[5], bank[7]

        xin = [sem(f"x_in{i}") for i in range(4)]
        ffn_raw = [sem(f"ffn_raw{i}") for i in range(3)]
        attn_raw, hs_in, tab_in = sem("attn_raw"), sem("hs_in"), sem("tab_in")
        consts = sem("consts_ready")
        neghalf = sem("neghalf_ready")
        f_part = [sem(f"f_partial{i}") for i in range(3)]
        tern = [sem(f"ternary_ready{i}") for i in range(3)]
        f_tot, f_sc, tern_a, less = (sem(n) for n in ("f_total", "f_scales", "tern_first_cmp", "tern_cmp"))
        a_sc_dve = sem("a_scale_steps")
        hs_mul, a_part, a_tot, a_sc = sem("wo_head_scaled"), sem("a_partial"), sem("a_total"), sem("a_scales")
        w_hi, w_ready = sem("w_hi"), sem("attn_weights_ready")
        ln_st, ln_mv, ln_ve, ln_rs, ln_xn, ln_t, ln_xh, ln_xl = (
            sem("ln_" + n) for n in ("stats", "meanvar", "vareps", "rstd", "xn", "turned", "xh", "xl"))
        ff = [{n: sem(f"{n}_{l}") for n in ("u_done", "g_done", "silu_done", "h_done", "hh_done", "hl_done",
                                            "down_done", "y_done", "x_done")} for l in range(2)]
        half_done, out_done = sem("last_sums_half_done"), sem("out_done")
        proj, swap, mul, add, qk_hi, qk_lo, v_hi, v_lo = (
            sem(n) for n in ("proj_done", "rope_swapped", "rope_mul", "rope_add", "qk_hi", "qk_lo", "v_hi", "v_lo"))
        s_done, mx, ex, rcp, pn = (
            sem(n) for n in ("scores_done", "max_done", "exp_done", "recip_done", "probs_normed"))
        pt_t = [sem(f"probs_turned{i}") for i in range(2)]
        row_t, p_hi, p_lo, o_done, oh, ol = (
            sem(n) for n in ("rows_turned", "probs_hi", "probs_lo", "o_done", "o_hi", "o_lo"))
        w_done, x2, a_st, a_mv, a_ve, a_rs, a_xn, a_xh, a_xl = (
            sem("at_" + n) for n in ("wo_done", "x2", "stats", "meanvar", "vareps", "rstd", "xn", "xh", "xl"))

        xv = x.rearrange("b (t p) d -> p (b t) d", p=P)
        ov = out.rearrange("b (t p) d -> p (b t) d", p=P)
        XV = X[:, :].rearrange("p (j d) -> p j d", d=D)

        def wait(eng, s, value):
            if not isinstance(value, int) or value > 0:
                eng.wait_ge(s, value)

        def wait_alone(eng, s, value):
            if not isinstance(value, int):
                value = eng.to_reg(value)
                eng.wait_ge(consts, 5)
            eng.wait_ge(s, value)

        BLOCKS = ((0, 128), (128, 384))
        flat = lambda a: a[:, :, :].rearrange("p c n -> p (c n)")
        CUTS = [(RQ, WQH, WQL, 1024, 0), (RK, WKH, WKL, 256, 1), (RV, WVH, WVL, 256, 2), (RO, WOH, WOL, 1024, 3)]
        CUT0 = 3
        LAG = 3
        TERNARY = {-1: [(0, 0), (1, 0)], 0: [(0, 1), (1, 1)], 1: [(0, 2), (2, 0)], 2: [(1, 2)], 3: [(0, 3), (2, 1)],
                   4: [(1, 3)], 5: [(2, 2)], 6: [(2, 3)]}
        LESS = {-1: [(0, 1), (1, 1)], 0: [(0, 2), (2, 0)], 1: [(1, 2), (0, 3)], 2: [(2, 1), (1, 3)], 3: [(2, 2)], 4: [(2, 3)]}
        LESS_ORDER = [q for f in LESS for q in LESS[f]]

        def quarter(i, q):
            raw, t = ((RU, TU), (RG, TG), (RD, TD))[i]
            if i < 2:
                cut = lambda a: a[:, :, q * 256:(q + 1) * 256]
                return cut(raw.rearrange("p (c e) -> p c e", c=DC)), cut(t)
            return raw[:, q * 512:(q + 1) * 512], flat(t)[:, q * 512:(q + 1) * 512]

        def real(b, i, lag):
            return not isinstance(b, int) or 0 <= PAIRS * b + i - lag < STEPS

        def ln_jobs(n):
            if isinstance(n, int) and n == 0:
                return [(-1, 2, 5, 1, 1)]
            if isinstance(n, int) and n == TILES - 1:
                return [(4, 5, 6, 2 * n, n - 1)]
            return [(0, 1, 2, 2 * n, n + 1), (4, 5, 6, 2 * n + 1, n - 1)]

        def ends(b):
            return None if isinstance(b, int) and not 0 <= b - 2 < BATCH else b - 2

        def batches(eng, body):
            body(0)
            body(1)
            with eng.Fori(2, BATCH) as b:
                body(b)
            body(BATCH)

        def for_tiles(eng, body):
            body(0)
            with eng.Fori(1, TILES) as n:
                body(n)

        block = ctx.enter_context(nc.Block())

        @block.sync
        def _(sp):
            sp.dma_start(XV[:, 0:4, :], xv[:, 0:4, :]).then_inc(xin[0], 16)
            sp.dma_start(RU, wu.rearrange("(c p) e -> p c e", p=P)).then_inc(ffn_raw[0], 16)
            sp.dma_start(RG, wg.rearrange("(c p) e -> p c e", p=P)).then_inc(ffn_raw[1], 16)
            sp.dma_start(RD, wd.rearrange("(c p) d -> p c d", p=P)).then_inc(ffn_raw[2], 16)
            sp.dma_start(XV[:, 4:8, :], xv[:, 4:8, :]).then_inc(xin[1], 16)
            sp.dma_start(XV[:, 8:12, :], xv[:, 8:12, :]).then_inc(xin[2], 16)
            sp.dma_start(RK, wk.rearrange("(c p) e -> p c e", p=P)).then_inc(attn_raw, 16)
            sp.dma_start(RV, wv.rearrange("(c p) e -> p c e", p=P)).then_inc(attn_raw, 16)
            sp.dma_start(RQ, wq.rearrange("(c p) e -> p c e", p=P)).then_inc(attn_raw, 16)
            sp.dma_start(RO, wo.rearrange("(h p) d -> p h d", p=P)).then_inc(attn_raw, 16)
            sp.wait_ge(tern[0], 4)
            sp.wait_ge(tern[1], 4)
            sp.dma_start(XV[:, 12:32, :], xv[:, 12:32, :]).then_inc(xin[3], 16)
            def turn_probs(par):
                sp.dma_start_transpose(PT[:, par, :, :], PR[:, par, :]).then_inc(pt_t[par], 16)

            for e in range(2):
                sp.wait_ge(p_lo, e + 1)
                turn_probs(e)
            with sp.Fori(1, STEPS // 2) as m:
                for par in range(2):
                    ready, used = sp.to_reg(2 * m + par + 1), sp.to_reg(2 * m + par - 1)
                    sp.wait_ge(consts, 5)
                    sp.wait_ge(p_lo, ready)
                    sp.wait_ge(o_done, used)
                    turn_probs(par)
            with sp.Fori(0, TILES - 1) as n:
                sp.wait_ge(ff[1]["x_done"], n * SUB + SUB)
                sp.dma_start(ov[:, bass.ds(n * SUB, SUB), :], XV[:, bass.ds(n * SUB, SUB), :]).then_inc(out_done, 16)
            for half in range(2):
                j = TOK // P - SUB + 2 * half
                sp.wait_ge(ff[1]["x_done"], j + 2)
                sp.dma_start(ov[:, j:j + 2, :], XV[:, j:j + 2, :]).then_inc(out_done, 16)
            sp.wait_ge(out_done, 16 * (TILES + 1))

        @block.gpsimd
        def _(gp):
            gp.memset(NEGHALF[:, :], -0.5).then_inc(neghalf, 1)
            gp.memset(PMAX[:, :], 0.0).then_inc(consts, 1)
            gp.memset(IDF[:, :], 0.0).then_inc(consts, 1)
            gp.memset(MASK[:, :], 0.0).then_inc(consts, 1)
            gp.wait_ge(consts, 3)
            gp.affine_select(out=IDF[:, :], in_=IDF[:, :], compare_op=ALU.not_equal, fill=1.0, base=0,
                             pattern=[[-1, P]], channel_multiplier=1).then_inc(consts, 1)
            gp.affine_select(out=MASK[:, P:2 * P], in_=MASK[:, P:2 * P], compare_op=ALU.is_ge, fill=MASKED, base=0,
                             pattern=[[-1, P]], channel_multiplier=1).then_inc(consts, 1)

            def rstd(q):
                wait(gp, ln_xn, 4 * q)
                wait_alone(gp, ln_mv, 4 * q + 4)
                gp.tensor_scalar(VE[:, :], MV[:, :, 1], 1.0 / LNS ** 2, EPS / LNS ** 2, ALU.mult, ALU.add).then_inc(ln_ve, 1)
                gp.wait_ge(ln_ve, q + 1)
                gp.tensor_tensor(RSTD[:, :], VE[:, :], NEGHALF[:, :], ALU.pow).then_inc(ln_rs, 1)

            def compare(f):
                for i, q in LESS[f]:
                    gp.wait_ge(f_sc, (1, 4, 6)[i])
                    raw, t = quarter(i, q)
                    gp.tensor_scalar(t, raw, FNEG[:, i:i + 1], None, ALU.is_lt).then_inc(less, 1)

            def ffn(layer, n, jobs):
                s = ff[layer]
                for f in range(FC):
                    gp.wait_ge(s["hh_done"], FC * n + f + 1)
                    gp.tensor_tensor(HL[:, f % 4, :], H32[:, f % 2, :], HH[:, f % 4, :], ALU.subtract).then_inc(s["hl_done"], 1)
                    if layer == 0 and isinstance(n, int) and n == 0 and f in LESS:
                        compare(f)
                    for f0, _, _, q, _ in jobs:
                        if f == f0:
                            rstd(q)
                    if layer == 0 and isinstance(n, int) and (n, f) == (2, 6):
                        gp.wait_ge(a_part, 11)
                        gp.partition_all_reduce(AMAX[:, :], PM4[:, :], P, bass.bass_isa.ReduceOp.max).then_inc(a_tot, 1)
                    if layer == 1 and isinstance(n, int) and n == 0 and f == 0:
                        rows_rstd(BATCH - 1)

            def rope_add(r, m):
                wait(gp, qk_lo, r - 1)
                gp.wait_ge(mul, r + 1)
                gp.tensor_tensor(QK[:, m, :], M1[:, m, :], M2[:, m, :], ALU.add).then_inc(add, 1)

            def rope_lo(r, m, hi, lo):
                gp.wait_ge(qk_hi, r + 1)
                gp.tensor_tensor(lo, QK[:, m, :], hi, ALU.subtract).then_inc(qk_lo, 1)

            def rows_rstd(e):
                wait_alone(gp, a_mv, 2 * e + 2)
                gp.tensor_scalar(VE[:, 0:2], MV[:, 0:2, 1], 1.0 / LNS ** 2, EPS / LNS ** 2, ALU.mult, ALU.add).then_inc(a_ve, 1)
                gp.wait_ge(a_ve, e + 1)
                gp.tensor_tensor(RSTD[:, 0:2], VE[:, 0:2], NEGHALF[:, 0:2], ALU.pow).then_inc(a_rs, 1)

            def norm(e, par):
                wait_alone(gp, rcp, e + 1)
                for hh in range(2):
                    for blk, (lo, hi) in enumerate(BLOCKS):
                        c, lo, hi = 2 * hh + blk, 384 * hh + lo, 384 * hh + hi
                        last = gp.tensor_scalar(EX[:, par, lo:hi], EX[:, par, lo:hi], RI[:, par, c:c + 1], PS, ALU.mult, ALU.mult)
                last.then_inc(pn, 1)

            def batch(b):
                for i in range(PAIRS):
                    g, k = divmod(i, 4)
                    u, t = 2 * b + g, PAIRS * b + i
                    r, m = 5 * u + 1 + k, (5 * g + 1 + k) % 2
                    if real(b, i, 0):
                        if k == 0:
                            if isinstance(b, int) and b + i == 0:
                                gp.wait_ge(ff[0]["down_done"], FC * TILES - 2)
                            rope_add(r - 1, 1 - m)
                        if isinstance(b, int) and b + i == 0:
                            gp.wait_ge(ff[0]["down_done"], FC * TILES)
                        rope_add(r, m)
                    if real(b, i, 2):
                        norm(t - 2, i % 2)
                    if real(b, i, 0):
                        if k == 0:
                            rope_lo(r - 1, 1 - m, KH[:, g, :], KL[:, g, :])
                        rope_lo(r, m, QH[:, i % 2, :], QL[:, i % 2, :])
                    if i == 0 and ends(b) is not None:
                        rows_rstd(ends(b))
                    if isinstance(b, int) and (b, i) == (0, 1):
                        rstd(2 * TILES - 1)

            gp.wait_ge(neghalf, 1)
            rstd(0)
            for i in range(3):
                if i == 2:
                    compare(-1)
                gp.wait_ge(f_part[i], 1)
                gp.partition_all_reduce(FTOT[:, i:i + 1], PSUMS[:, i:i + 1], P, bass.bass_isa.ReduceOp.add).then_inc(f_tot, 1)
            rstd(1)
            for n in range(CUT0):
                ffn(0, n, ln_jobs(n))
            with gp.Fori(CUT0, TILES - 1) as n:
                ffn(0, n, ln_jobs(n))
            ffn(0, TILES - 1, ln_jobs(TILES - 1))
            batches(gp, batch)
            for_tiles(gp, lambda n: ffn(1, n, []))

        @block.scalar
        def _(act):
            act.dma_start(HS[:, :], hscale).then_inc(hs_in, 16)
            act.dma_start(COS[:, :], cos_t).then_inc(tab_in, 16)
            act.dma_start(SIN[:, :], sin_t).then_inc(tab_in, 16)

            def ln_hi(q, tile, banks=TB):
                for c in range(DC):
                    act.wait_ge(ln_t, 2 * q + c + 1)
                    act.copy(XH[:, c, bass.ds(tile * TILE, TILE)], banks[c][:, :]).then_inc(ln_xh, 1)

            def ffn(layer, n, jobs):
                s = ff[layer]
                for f in range(FC):
                    j = FC * n + f
                    act.wait_ge(s["u_done"], j + 1)
                    wait(act, s["h_done"], j - 1)
                    act.activation(SG[:, f % 2, :], UB[f % 2][:, :], ACT.Silu, scale=SU16[:, 0:1]).then_inc(s["silu_done"], 1)
                    if layer == 0 and isinstance(n, int) and n + f == 0:
                        act.wait_ge(ffn_raw[2], 16)
                        act.activation(flat(TD), RD, ACT.Abs, accum_out=PSUMS[:, 2:3]).then_inc(f_part[2], 1)
                    act.wait_ge(s["h_done"], j + 1)
                    wait(act, s["down_done"], j - 3)
                    act.copy(HH[:, f % 4, :], H32[:, f % 2, :]).then_inc(s["hh_done"], 1)
                    for _, _, ft, q, tile in jobs:
                        if f == ft:
                            ln_hi(q, tile)
                    if layer == 0:
                        weights(n, f)
                    if layer == 1 and isinstance(n, int) and n == 0 and f in (3, 5):
                        rows_hi(BATCH - 1, (f - 3) // 2)

            def weights(n, f):
                if isinstance(n, int) and n == 1:
                    if f == 0:
                        act.wait_ge(hs_in, 16)
                        act.wait_ge(attn_raw, 64)
                    for h in range(2 * f, 2 * f + 2):
                        act.mul(RO[:, h * D:(h + 1) * D], RO[:, h * D:(h + 1) * D], HS[:, h:h + 1]).then_inc(hs_mul, 1)
                if not isinstance(n, int) and f in (1, 3, 4, 5):
                    act.wait_ge(a_sc, 1)
                    raw, hi, _, size, c = CUTS[(1, 3, 4, 5).index(f)]
                    cols = bass.ds((n - CUT0) * size, size)
                    act.mul(flat(hi)[:, cols], raw[:, cols], AFAC[:, c:c + 1]).then_inc(w_hi, 1)

            def rows_hi(e, j):
                act.wait_ge(row_t, 2 * e + j + 1)
                act.copy(XH[:, :, bass.ds(e * SEQ + j * P, P)], RB[:, 0:D].rearrange("p (c n) -> p c n", c=DC)).then_inc(a_xh, 1)

            act.wait_ge(neghalf, 1)
            act.activation(WARM[:, 0:1], NEGHALF[:, 0:1], ACT.Silu)
            act.wait_ge(ffn_raw[0], 16)
            act.activation(flat(TU), RU, ACT.Abs, accum_out=PSUMS[:, 0:1]).then_inc(f_part[0], 1)
            ln_hi(0, 0)
            act.wait_ge(ffn_raw[1], 16)
            act.activation(flat(TG), RG, ACT.Abs, accum_out=PSUMS[:, 1:2]).then_inc(f_part[1], 1)
            act.wait_ge(f_sc, 1)
            for n in range(CUT0):
                ffn(0, n, ln_jobs(n))
            with act.Fori(CUT0, TILES - 1) as n:
                ffn(0, n, ln_jobs(n))
            ffn(0, TILES - 1, ln_jobs(TILES - 1))

            def rope_swap(r, m):
                wait(act, add, r - 1)
                for d, s in ((0, 64), (64, 0)):
                    last = act.copy(M2[d:d + 64, m, :], PJ[m][s:s + 64, :])
                last.then_inc(swap, 1)

            def batch(b):
                for i in range(PAIRS):
                    g, k = divmod(i, 4)
                    u, t = 2 * b + g, PAIRS * b + i
                    if real(b, i, 0):
                        r, m = 5 * u + 1 + k, (5 * g + 1 + k) % 2
                        if k == 0:
                            act.wait_ge(proj, 6 * u + 1)
                            if isinstance(b, int) and b + i == 0:
                                act.wait_ge(ff[0]["hl_done"], FC * TILES - 1)
                            rope_swap(r - 1, 1 - m)
                        act.wait_ge(proj, 6 * u + 2 + k)
                        if isinstance(b, int) and b + i == 0:
                            act.wait_ge(ff[0]["hl_done"], FC * TILES)
                        rope_swap(r, m)
                        if isinstance(b, int) and b + i == 0:
                            act.activation(WARM[:, 1:2], NEGHALF[:, 0:1], ACT.Exp)
                    if real(b, i, 2):
                        e, par = t - 2, i % 2
                        wait(act, p_lo, e - 1)
                        for hh in range(2):
                            act.wait_ge(mx, 2 * e + hh + 1)
                            for blk, (lo, hi) in enumerate(BLOCKS):
                                c = 2 * hh + blk
                                last = act.activation(EX[:, par, 384 * hh + lo:384 * hh + hi], SBK[hh][:, lo:hi], ACT.Exp, bias=NM[:, par, c:c + 1],
                                                      scale=-1.0, accum_out=RS[:, par, c:c + 1])
                            last.then_inc(ex, 1)
                    if real(b, i, 3):
                        e, par = t - 3, (i - 3) % 2
                        act.wait_ge(pn, e + 1)
                        wait(act, pt_t[par], 16 * (4 * b + (i - 3) // 2))
                        act.copy(PR[:, par, 0:768], EX[:, par, :]).then_inc(p_hi, 1)
                    if k == 3 and real(b, i, 0):
                        act.wait_ge(proj, 6 * u + 6)
                        wait(act, o_done, 4 * u - 4)
                        act.mul(VH[:, g, :], RB[:, :], VS).then_inc(v_hi, 1)
                    if real(b, i, 5):
                        e = t - 5
                        act.wait_ge(o_done, e + 1)
                        h = 2 * ((i - 5) % PAIRS) * SEQ
                        act.mul(OH[:, h:h + 2 * SEQ], OB[(i - 5) % 2][:, :], 1.0 / PS).then_inc(oh, 1)
                    if i in (2, 4) and ends(b) is not None:
                        rows_hi(ends(b), (i - 2) // 2)
                    if real(b, i, 0):
                        if k == 0:
                            act.wait_ge(add, r)
                            wait(act, s_done, 8 * u - 8)
                            act.copy(KH[:, g, :], QK[:, 1 - m, :]).then_inc(qk_hi, 1)
                        act.wait_ge(add, r + 1)
                        wait(act, s_done, 2 * t - 2)
                        act.copy(QH[:, i % 2, :], QK[:, m, :]).then_inc(qk_hi, 1)
                    if isinstance(b, int) and (b, i) == (0, 3):
                        ln_hi(2 * TILES - 1, TILES - 1, YB)

            batches(act, batch)

            for_tiles(act, lambda n: ffn(1, n, []))

        @block.tensor
        def _(pe):
            def turn(q, rows=XN, banks=TB):
                wait(pe, ln_xl, 2 * q)
                for s in range(SUB):
                    pe.wait_ge(ln_xn, 4 * q + s + 1)
                for c in range(DC):
                    for s in range(SUB):
                        last = pe.transpose(banks[c][:, s * P:(s + 1) * P], rows[:, s, c * P:(c + 1) * P], IDF[:, :])
                    last.then_inc(ln_t, 1)

            def up(layer, n, f):
                s = ff[layer]
                j = FC * n + f
                cols = bass.ds(n * TILE, TILE)
                making = layer == 0 and isinstance(n, int) and n == 0 and f % 2 == 0
                if making:
                    pe.wait_ge(tern[0], f // 2 + 1)
                wait(pe, s["silu_done"], j - 1)
                for a, xs in enumerate((XH, XL)):
                    if making and f == 0:
                        pe.wait_ge((ln_xh, ln_xl)[a], 2)
                    for c in range(DC):
                        last = pe.matmul(UB[f % 2][:, :], TU[:, c, f * P:(f + 1) * P], xs[:, c, cols],
                                         start=a + c == 0, stop=a + c == 2)
                last.then_inc(s["u_done"], 1)
                if making:
                    pe.wait_ge(tern[1], f // 2 + 1)
                wait(pe, s["h_done"], j - 1)
                for a, xs in enumerate((XH, XL)):
                    for c in range(DC):
                        last = pe.matmul(GB[f % 2][:, :], TG[:, c, f * P:(f + 1) * P], xs[:, c, cols],
                                         start=a + c == 0, stop=a + c == 2)
                last.then_inc(s["g_done"], 1)

            def down(layer, n, f):
                s = ff[layer]
                j = FC * n + f
                pe.wait_ge(s["hl_done"], j + 1)
                if f == 0:
                    wait(pe, s["x_done"], SUB * n)
                if isinstance(n, int) and n == 0:
                    if layer == 0 and f % 2 == 0:
                        pe.wait_ge(tern[2], f // 2 + 1)
                    if layer == 1 and f == 0:
                        pe.wait_ge(x2, 2 * BATCH)
                for sub in range(SUB):
                    for a, hs in enumerate((HH, HL)):
                        last = pe.matmul(YB[sub // 2][:, (sub % 2) * D:(sub % 2 + 1) * D], hs[:, f % 4, sub * P:(sub + 1) * P],
                                         TD[:, f, :], start=f == 0 and a == 0 and sub % 2 == 0,
                                         stop=f == FC - 1 and a == 1, skip_group_check=True)
                    if layer == 1 and isinstance(n, int) and (n, f, sub) == (TILES - 1, FC - 1, 1):
                        last.then_inc(half_done, 1)
                last.then_inc(s["down_done"], 1)

            def pairs(dst, lh, ll, rh, rl, n, start, stop):
                todo = [(l, r, c) for l, r in ((lh, rh), (lh, rl), (ll, rh)) for c in range(n)]
                for x, (l, r, c) in enumerate(todo):
                    last = pe.matmul(dst, l(c), r(c), start=start and x == 0, stop=stop and x == len(todo) - 1,
                                     skip_group_check=True)
                return last

            def project_qk(dst, wh, wl, h0, b):
                cols = bass.ds(b * SEQ, SEQ)
                for hh in range(2):
                    w = slice((h0 + hh) * DH, (h0 + hh + 1) * DH)
                    last = pairs(dst[:, hh * SEQ:(hh + 1) * SEQ], lambda c: wh[:, c, w], lambda c: wl[:, c, w],
                                 lambda c: XH[:, c, cols], lambda c: XL[:, c, cols], DC, hh == 0, hh == 1)
                last.then_inc(proj, 1)

            def ffn(layer, n, jobs, prev):
                for f in range(FC):
                    up(layer, n, f)
                    if layer == 0 and isinstance(n, int) and (n, f) == (TILES - 1, FC - 1):
                        pe.wait_ge(w_ready, 4 * len(CUTS))
                        pe.wait_ge(ff[0]["silu_done"], FC * TILES - 1)
                        project_qk(PJ[0], WKH, WKL, 0, 0)
                    if f >= LAG:
                        down(layer, n, f - LAG)
                    elif prev:
                        down(layer, n - 1, f + FC - LAG)
                    for _, _, ft, q, _ in jobs:
                        if f == ft:
                            turn(q)
                    if layer == 1 and isinstance(n, int) and n == 0 and f in (3, 5):
                        turn_rows(BATCH - 1, (f - 3) // 2)

            pe.wait_ge(consts, 5)
            turn(0)
            ffn(0, 0, ln_jobs(0), False)
            for n in range(1, CUT0):
                pe.wait_ge(ln_xl, 4 * n if n == 1 else 4 * n - 2)
                ffn(0, n, ln_jobs(n), True)
            with pe.Fori(CUT0, TILES - 1) as n:
                pe.wait_ge(ln_xl, 4 * n - 2)
                ffn(0, n, ln_jobs(n), True)
            pe.wait_ge(ln_xl, 4 * TILES - 6)
            ffn(0, TILES - 1, ln_jobs(TILES - 1), True)

            def project_v(dst, b, g):
                for j in range(2):
                    rows = bass.ds(b * SEQ + j * P, P)
                    w = slice(g * 256, g * 256 + 256)
                    last = pairs(dst[:, j * 256:(j + 1) * 256], lambda c: XH[:, c, rows], lambda c: XL[:, c, rows],
                                 lambda c: WVH[:, c, w], lambda c: WVL[:, c, w], DC, j == 0, j == 1)
                last.then_inc(proj, 1)

            def scores(t, i, u):
                pe.wait_ge(qk_lo, 5 * u + i % 4 + 2)
                g, kv = i // 4, i % 4 // 2
                for hh in range(2):
                    wait(pe, ex, 2 * t + hh - 1)
                    bk = SBK[hh]
                    for blk, (lo, hi) in enumerate(BLOCKS):
                        q = [a[:, i % 2, hh * SEQ + blk * P:hh * SEQ + (blk + 1) * P] for a in (QH, QL)]
                        k = [a[:, g, kv * SEQ:kv * SEQ + hi - lo] for a in (KH, KL)]
                        last = pairs(bk[:, lo:hi], lambda c: q[0], lambda c: q[1], lambda c: k[0], lambda c: k[1], 1, blk == 0, blk == 1)
                    last.then_inc(s_done, 1)

            def values(t, i, u, done):
                g, kv = i // 4, i % 4 // 2
                pe.wait_ge(v_lo, u + 1)
                wait(pe, ol, t - 1)
                ob = OB[i % 2]
                pe.wait_ge(pt_t[i % 2], done)
                v = [[a[:, g, (2 * j + kv) * DH:(2 * j + kv + 1) * DH] for j in range(2)] for a in (VH, VL)]
                for hh in range(2):
                    ph, pl = (PT[:, i % 2, b0 + 3 * hh:b0 + 3 * hh + 3, :].rearrange("p k n -> p (k n)") for b0 in (0, 6))
                    o = hh * SEQ
                    pairs(ob[:, o:o + 256], lambda c: v[0][0], lambda c: v[1][0],
                          lambda c: ph[:, 0:256], lambda c: pl[:, 0:256], 1, hh == 0, False)
                    last = pairs(ob[:, o + 128:o + 256], lambda c: v[0][1], lambda c: v[1][1],
                                 lambda c: ph[:, 256:384], lambda c: pl[:, 256:384], 1, False, hh == 1)
                last.then_inc(o_done, 1)

            def turn_rows(e, j):
                if isinstance(e, int) or j:
                    wait(pe, a_xl, 2 * e + j)
                pe.wait_ge(a_xn, 2 * e + j + 1)
                for c in range(DC):
                    last = pe.transpose(RB[:, c * P:(c + 1) * P], XN2[:, j, c * P:(c + 1) * P], IDF[:, :])
                last.then_inc(row_t, 1)

            def output(b, i):
                pe.wait_ge(ol, PAIRS * (b - 1) + i + 1)
                if i == 0:
                    wait(pe, x2, 2 * (b - 1))
                for h in (2 * i, 2 * i + 1):
                    for j in range(2):
                        rows = slice(h * SEQ + j * P, h * SEQ + (j + 1) * P)
                        last = pairs(WB[:, j * 256:(j + 1) * 256], lambda c: OH[:, rows], lambda c: OL[:, rows],
                                     lambda c: WOH[:, h, :], lambda c: WOL[:, h, :], 1, h == 0 and j == 0, h == HEADS - 1 and j == 1)
                if i == PAIRS - 1:
                    last.then_inc(w_done, 1)

            def batch(b):
                for i in range(PAIRS):
                    g, k = divmod(i, 4)
                    u, t = 2 * b + g, PAIRS * b + i
                    unit = lambda lag: 2 * b + (i - lag) // 4
                    if real(b, i, 0):
                        r, m = 5 * u + 1 + k, (5 * g + 1 + k) % 2
                        if k == 0 and (not isinstance(b, int) or b + i > 0):
                            wait(pe, mul, r - 2)
                            project_qk(PJ[1 - m], WKH, WKL, 2 * g, b)
                        wait(pe, mul, r - 1)
                        if isinstance(b, int) and b + i == 0:
                            pe.wait_ge(ff[0]["silu_done"], FC * TILES)
                        project_qk(PJ[m], WQH, WQL, 8 * g + 2 * k, b)
                        if isinstance(b, int) and b + i == 0:
                            for f in range(FC - LAG, FC):
                                down(0, TILES - 1, f)
                    if real(b, i, 2):
                        scores(t - 2, (i - 2) % PAIRS, unit(2))
                    if isinstance(b, int) and b == BATCH:
                        for pair in {2: (2, 3), 3: (4,), 4: (5,)}.get(i, ()):
                            output(b, pair)
                    if real(b, i, 5):
                        if isinstance(b, int) and (b, i) == (0, 5):
                            pe.wait_ge(ln_xl, 4 * TILES)
                        values(t - 5, (i - 5) % PAIRS, unit(5), 16 * (4 * b + (i - 5) // 2 + 1))
                    if real(b, i, 0) and k == 3:
                        wait(pe, v_lo, u)
                        if ends(b) is not None:
                            pe.wait_ge(a_xl, 2 * ends(b) + 1 + g)
                        elif isinstance(b, int) and b == 0:
                            pe.wait_ge(ln_xl, 4 * TILES - 2)
                        project_v(RB, b, g)
                    if i in (2, 4) and ends(b) is not None:
                        values_read = 2 * b + (i - 2) // 2
                        pe.wait_ge(v_lo, min(values_read, 2 * BATCH) if isinstance(b, int) else values_read)
                        turn_rows(ends(b), (i - 2) // 2)
                    if isinstance(b, int) and (b, i) == (0, 3):
                        turn(2 * TILES - 1, XN7, YB)
                    if not isinstance(b, int) or 0 < b < BATCH or b == BATCH and i in (0, 1, 6, 7):
                        output(b, i)

            batches(pe, batch)

            ffn(1, 0, [], False)
            with pe.Fori(1, TILES) as n:
                ffn(1, n, [], True)
            for f in range(FC - LAG, FC):
                down(1, TILES - 1, f)

        @block.vector
        def _(ve):
            def stats(q, tile):
                for s in range(SUB):
                    ve.bn_stats(ST[:, s, :], X[:, bass.ds(tile * (SUB * D) + s * D, D)]).then_inc(ln_st, 1)
                for s in range(SUB):
                    wait_alone(ve, ln_st, 4 * q + s + 1)
                    ve.bn_aggr(MV[:, s, :], ST[:, s, :]).then_inc(ln_mv, 1)

            def center(q, tile, rows=XN):
                ve.wait_ge(ln_rs, q + 1)
                wait(ve, ln_t, 2 * q)
                for s in range(SUB):
                    ve.tensor_scalar(rows[:, s, :], X[:, bass.ds(tile * (SUB * D) + s * D, D)], MV[:, s, 0:1],
                                     RSTD[:, s:s + 1], ALU.subtract, ALU.mult).then_inc(ln_xn, 1)

            def ln_lo(q, tile, banks=TB):
                for c in range(DC):
                    cols = bass.ds(tile * TILE, TILE)
                    ve.wait_ge(ln_xh, 2 * q + c + 1)
                    ve.tensor_tensor(XL[:, c, cols], banks[c][:, :], XH[:, c, cols], ALU.subtract).then_inc(ln_xl, 1)

            def residual(layer, tile):
                s = ff[layer]
                last = layer == 1 and isinstance(tile, int) and tile == TILES - 1
                if last:
                    ve.wait_ge(half_done, 1)
                else:
                    ve.wait_ge(s["down_done"], FC * tile + FC)
                for sub in range(SUB):
                    if last and sub == 2:
                        ve.wait_ge(s["down_done"], FC * TILES)
                    rows = X[:, bass.ds(tile * (SUB * D) + sub * D, D)]
                    ve.scalar_tensor_tensor(rows, YB[sub // 2][:, (sub % 2) * D:(sub % 2 + 1) * D], CY[:, 0:1], rows,
                                            ALU.mult, ALU.add).then_inc(s["x_done"], 1)

            def ffn(layer, n, jobs, prev):
                s = ff[layer]
                for f in range(FC):
                    j = FC * n + f
                    ve.wait_ge(s["silu_done"], j + 1)
                    ve.wait_ge(s["g_done"], j + 1)
                    wait(ve, s["hl_done"], j - 1)
                    ve.scalar_tensor_tensor(H32[:, f % 2, :], SG[:, f % 2, :], CS[:, 0:1], GB[f % 2][:, :],
                                            ALU.mult, ALU.mult).then_inc(s["h_done"], 1)
                    if layer == 0 and isinstance(n, int) and n == 0 and f in TERNARY:
                        ternary(f)
                    if layer == 1 and isinstance(n, int) and n == 0:
                        last_rows(f)
                    for f0, _, _, q, tile in jobs:
                        if f == f0:
                            if f0 == 4:
                                wait_alone(ve, s["x_done"], SUB * n)
                            stats(q, tile)
                    if f == LAG - 1 and prev:
                        residual(layer, n - 1)
                    for _, fc, ft, q, tile in jobs:
                        if f == fc:
                            center(q, tile)
                        if f == ft + 1:
                            ln_lo(q, tile)
                    if layer == 0:
                        weights(n, f)

            def weights(n, f):
                if isinstance(n, int):
                    maxima = {(0, 5): (1, 0), (0, 6): (2, 0), (0, 7): (0, 0), (1, 2): (0, 1), (1, 3): (0, 2), (1, 6): (0, 3),
                              (1, 7): (3, 0), (2, 2): (3, 1), (2, 3): (3, 2), (2, 6): (3, 3)}
                    if (n, f) in maxima:
                        w, piece = maxima[n, f]
                        ve.wait_ge(attn_raw, 64)
                        if w == 3:
                            ve.wait_ge(hs_mul, 4 * piece + 4)
                        ve.tensor_reduce(PMAX[:, 4 * piece + w:4 * piece + w + 1], (RQ, RK, RV, RO)[w][:, piece * 1024:(piece + 1) * 1024],
                                         AX.X, ALU.max, apply_absolute_value=True).then_inc(a_part, 1)
                    if (n, f) == (2, 6):
                        ve.wait_ge(a_part, 10)
                        ve.tensor_reduce(PM4[:, :], PMAX[:, :].rearrange("p (j w) -> p w j", w=4), AX.X, ALU.max).then_inc(a_part, 1)
                    if (n, f) == (2, 7):
                        scales()
                elif f in (2, 4, 5, 6):
                    i = (2, 4, 5, 6).index(f)
                    raw, hi, lo, size, c = CUTS[i]
                    cols = bass.ds((n - CUT0) * size, size)
                    ve.wait_ge(w_hi, (n - CUT0) * len(CUTS) + i + 1)
                    ve.scalar_tensor_tensor(flat(lo)[:, cols], raw[:, cols], AFAC[:, c:c + 1],
                                            flat(hi)[:, cols], ALU.mult, ALU.subtract).then_inc(w_ready, 1)

            def ternary(f):
                for i, q in TERNARY[f]:
                    if f == -1:
                        ternary_scale(i)
                    raw, t = quarter(i, q)
                    if f == -1:
                        ve.tensor_scalar(t, raw, FNEG[:, i:i + 1], None, ALU.is_lt).then_inc(tern_a, 1)
                        ve.wait_ge(tern_a, i + 1)
                    else:
                        ve.wait_ge(less, LESS_ORDER.index((i, q)) + 1)
                    ve.scalar_tensor_tensor(t, raw, FHALF[:, i:i + 1], t, ALU.is_gt, ALU.subtract).then_inc(tern[i], 1)
                    if f == -1 and i == 0:
                        ln_lo(0, 0)
                if f == 0:
                    ternary_scale(2)

            def ternary_scale(i):
                ve.wait_ge(f_tot, i + 1)
                outs = [(FSC, 1.0), (FHALF, 0.5), (FNEG, -0.5)]
                if i == 0:
                    ve.tensor_scalar(SU16[:, :], FTOT[:, 0:1], 1.0 / (D * E) / LNS, 1e-8 / LNS, ALU.mult, ALU.add)
                for dst, by in outs:
                    last = ve.tensor_scalar(dst[:, i:i + 1], FTOT[:, i:i + 1], by / (D * E), by * 1e-8, ALU.mult, ALU.add)
                last.then_inc(f_sc, 1)
                ve.wait_ge(f_sc, (1, 4, 6)[i])
                if i == 0:
                    ve.reciprocal(FREC[:, 0:1], FSC[:, 0:1]).then_inc(f_sc, 1)
                    ve.wait_ge(f_sc, 2)
                    ve.tensor_scalar(CS[:, :], FREC[:, 0:1], HSC, None, ALU.mult).then_inc(f_sc, 1)
                if i == 1:
                    ve.tensor_tensor(CY0[:, :], FSC[:, 0:1], FSC[:, 1:2], ALU.mult).then_inc(f_sc, 1)
                    ve.wait_ge(f_sc, 5)
                if i == 2:
                    ve.tensor_tensor(CY[:, :], CY0[:, :], FSC[:, 2:3], ALU.mult).then_inc(f_sc, 1)
                    ve.wait_ge(f_sc, 7)

            def scales():
                ve.wait_ge(a_tot, 1)
                ve.tensor_scalar(AMG[:, :], AMAX[:, :], WMIN, None, ALU.max).then_inc(a_sc_dve, 1)
                ve.wait_ge(a_sc_dve, 1)
                ve.reciprocal(AREC[:, :], AMG[:, :])
                ve.tensor_tensor(SCQ0[:, :], AMG[:, 0:1], AMG[:, 1:2], ALU.mult)
                ve.tensor_tensor(CW0[:, :], AMG[:, 2:3], AMG[:, 3:4], ALU.mult).then_inc(a_sc_dve, 1)
                ve.wait_ge(a_sc_dve, 2)
                ve.tensor_scalar(SCQ[:, :], SCQ0[:, :], -DH ** -0.5 / (WTOP * LNS * QS) ** 2, None, ALU.mult)
                ve.tensor_scalar(CW[:, :], CW0[:, :], 1.0 / (VS * WTOP * LNS * WTOP), None, ALU.mult)
                ve.tensor_scalar(AFAC[:, :], AREC[:, :], WTOP, None, ALU.mult).then_inc(a_sc, 1)

            ve.wait_ge(xin[0], 16)
            stats(0, 0)
            ve.wait_ge(consts, 5)
            center(0, 0)
            ternary(-1)
            ve.wait_ge(xin[1], 16)
            ve.wait_ge(ln_rs, 1)
            stats(1, 1)

            for n in range(CUT0):
                if n > 0:
                    ve.wait_ge(xin[n + 1], 16)
                ffn(0, n, ln_jobs(n), n > 0)
            with ve.Fori(CUT0, TILES - 1) as n:
                ffn(0, n, ln_jobs(n), True)
            ffn(0, TILES - 1, ln_jobs(TILES - 1), True)

            ve.wait_ge(tab_in, 32)

            def rope_mul(r, m):
                wait(ve, add, r - 1)
                ve.wait_ge(swap, r + 1)
                two = lambda a: a.rearrange("p (h n) -> p h n", h=2)
                for dst, src, tb in ((M1[:, m, :], PJ[m][:, :], COS), (M2[:, m, :], M2[:, m, :], SIN)):
                    last = ve.tensor_tensor(two(dst), two(src), tb[:, :].unsqueeze(1).to_broadcast([P, 2, SEQ]), ALU.mult)
                last.then_inc(mul, 1)

            def batch(b):
                for i in range(PAIRS):
                    g, k = divmod(i, 4)
                    u, t = 2 * b + g, PAIRS * b + i
                    r, m = 5 * u + 1 + k, (5 * g + 1 + k) % 2
                    if i == 0 and ends(b) is not None:
                        rows_residual(ends(b))
                    if k == 0 and real(b, i, 0):
                        rope_mul(r - 1, 1 - m)
                    if real(b, i, 2):
                        e, par = t - 2, i % 2
                        for hh in range(2):
                            wait_alone(ve, s_done, 2 * e + hh + 1)
                            for blk, (lo, hi) in enumerate(BLOCKS):
                                c = 2 * hh + blk
                                last = ve.tensor_tensor_reduce(SBK[hh][:, lo:hi], SBK[hh][:, lo:hi], MASK[:, 256 - (hi - lo):256],
                                                               SCQ[:, 0:1], 3e38, ALU.add, ALU.min, NM[:, par, c:c + 1])
                            last.then_inc(mx, 1)
                    if real(b, i, 0):
                        rope_mul(r, m)
                    if isinstance(b, int) and (b, i) == (0, 0):
                        residual(0, TILES - 1)
                    if real(b, i, 6):
                        ve.wait_ge(oh, t - 5)
                        h = 2 * ((i - 6) % PAIRS) * SEQ
                        ve.scalar_tensor_tensor(OL[:, h:h + 2 * SEQ], OB[(i - 6) % 2][:, :], 1.0 / PS, OH[:, h:h + 2 * SEQ],
                                                ALU.mult, ALU.subtract).then_inc(ol, 1)
                    if real(b, i, 2):
                        ve.wait_ge(ex, 2 * e + 2)
                        wait(ve, pn, e - 1)
                        ve.reciprocal(RI[:, par, :], RS[:, par, :]).then_inc(rcp, 1)
                    if real(b, i, 3):
                        ve.wait_ge(p_hi, t - 2)
                        par = (i - 3) % 2
                        ve.tensor_tensor(PR[:, par, 768:1536], EX[:, par, :], PR[:, par, 0:768], ALU.subtract).then_inc(p_lo, 1)
                    if k == 3 and real(b, i, 0):
                        ve.wait_ge(v_hi, u + 1)
                        ve.scalar_tensor_tensor(VL[:, g, :], RB[:, :], VS, VH[:, g, :], ALU.mult, ALU.subtract).then_inc(v_lo, 1)
                    if i in (2, 4) and ends(b) is not None:
                        rows_lo(ends(b), (i - 2) // 2)
                    if i == 1 and ends(b) is not None:
                        rows_center(ends(b))
                    if i == 0 and ends(b) is not None:
                        rows_stats(ends(b))
                    if isinstance(b, int) and (b, i) == (0, 3):
                        ln_lo(2 * TILES - 1, TILES - 1, YB)
                    if isinstance(b, int) and (b, i) == (0, 1):
                        ve.wait_ge(ff[0]["x_done"], SUB * TILES)
                        stats(2 * TILES - 1, TILES - 1)
                    if isinstance(b, int) and (b, i) == (0, 2):
                        center(2 * TILES - 1, TILES - 1, XN7)

            def rows_residual(e):
                ve.wait_ge(w_done, e + 1)
                for j in range(2):
                    rows = X[:, bass.ds(e * (2 * D) + j * D, D)]
                    ve.scalar_tensor_tensor(rows, WB[:, j * 256:(j + 1) * 256], CW[:, 0:1], rows, ALU.mult, ALU.add).then_inc(x2, 1)

            def rows_stats(e):
                for j in range(2):
                    wait_alone(ve, x2, 2 * e + j + 1)
                    ve.bn_stats(ST[:, j, :], X[:, bass.ds(e * (2 * D) + j * D, D)]).then_inc(a_st, 1)
                for j in range(2):
                    wait_alone(ve, a_st, 2 * e + j + 1)
                    ve.bn_aggr(MV[:, j, :], ST[:, j, :]).then_inc(a_mv, 1)

            def rows_center(e):
                ve.wait_ge(a_rs, e + 1)
                for j in range(2):
                    ve.tensor_scalar(XN2[:, j, :], X[:, bass.ds(e * (2 * D) + j * D, D)], MV[:, j, 0:1], RSTD[:, j:j + 1],
                                     ALU.subtract, ALU.mult).then_inc(a_xn, 1)

            def rows_lo(e, j):
                cols = bass.ds(e * SEQ + j * P, P)
                ve.wait_ge(a_xh, 2 * e + j + 1)
                ve.tensor_tensor(XL[:, :, cols], RB[:, 0:D].rearrange("p (c n) -> p c n", c=DC), XH[:, :, cols],
                                 ALU.subtract).then_inc(a_xl, 1)

            def last_rows(f):
                if f == 1:
                    rows_center(BATCH - 1)
                if f in (4, 6):
                    rows_lo(BATCH - 1, (f - 4) // 2)

            batches(ve, batch)
            rows_residual(BATCH - 1)
            rows_stats(BATCH - 1)

            ffn(1, 0, [], False)
            with ve.Fori(1, TILES) as n:
                ffn(1, n, [], True)
            residual(1, TILES - 1)


def rotary_tables():
    inv = (1.0 / np.float32(10000.0) ** (np.arange(0, DH, 2, dtype=np.float32) / np.float32(DH))).astype(np.float32)
    ang = (np.arange(SEQ, dtype=np.float32)[None, :] * inv[:, None]).astype(np.float32)
    c, s = np.cos(ang), np.sin(ang)
    c, s = np.float32(QS) * c.astype(np.float32), np.float32(QS) * s.astype(np.float32)
    return np.concatenate([c, c]), np.concatenate([-s, s])


def kernel(**inputs):
    import concourse.bacc as bacc
    from concourse.bass_utils import run_bass_kernel_spmd as run

    nc = bacc.Bacc("TRN2", target_bir_lowering=False, num_devices=1)
    cos_t, sin_t = rotary_tables()
    get = lambda n: np.asarray(inputs[n])
    data = {
        "x": get("L0_attn_x"), "wq": get("L0_attn_Wq"), "wk": get("L0_attn_Wk"), "wv": get("L0_attn_Wv"),
        "wo": get("L0_attn_Wo"), "hscale": np.broadcast_to(get("L0_attn_head_scale").reshape(1, HEADS), (P, HEADS)),
        "wu": get("L0_ffn_W_up").T, "wg": get("L0_ffn_W_gate").T, "wd": get("L0_ffn_W_down").T,
        "cos_t": cos_t, "sin_t": sin_t,
    }
    arrays, args = {}, []
    for name, a in data.items():
        arrays["in_" + name] = np.ascontiguousarray(a)
        args.append(nc.dram_tensor("in_" + name, a.shape, mybir.dt.from_np(a.dtype), kind="ExternalInput").ap())
    args.append(nc.dram_tensor("out", (BATCH, SEQ, D), F32, kind="ExternalOutput").ap())
    program(nc, *args)
    return run(nc, [arrays], core_ids=[0]).results[0]["out"]
```
